# Optimizing a Trainium2 kernel written in Bass

```python
import numpy as np
import jax
import jax.numpy as jnp

def _softmax(x, axis=-1):
    return jax.nn.softmax(x, axis=axis)

def _gelu(x):
    return jax.nn.gelu(x, approximate=True)

def _silu(x):
    return jax.nn.silu(x)

def _sigmoid(x):
    return jax.nn.sigmoid(x)

def _layernorm(x, axis=-1, eps=1e-05):
    m = jnp.mean(x, axis=axis, keepdims=True)
    v = jnp.var(x, axis=axis, keepdims=True)
    return (x - m) / jnp.sqrt(v + eps)

def _scatter_add(tgt, idx, src, axis=0):
    return tgt.at[idx].add(src)

def _segment_sum(src, seg, n):
    return jax.ops.segment_sum(src, seg, n)
kernel_name = 'mk_adj_preln_d1_adj_r2_baf7d1'

def setup_inputs(seed: int=0):
    np.random.seed(seed)
    _w = jnp.asarray

    def _rec_inputs():
        import jax
        import jax.numpy as jnp
        _gk = jax.random.key(seed)
        x = -0.0005207 + 1.001 * jax.random.normal(jax.random.fold_in(_gk, 1), (8192, 128), jnp.float32)
        _a = jax.random.bernoulli(jax.random.fold_in(_gk, 2), 0.00195312, (8192, 8192))
        adj = _a.astype(jnp.int32)
        return (x, adj)
    x, adj = _rec_inputs()

    def _L0_gnn_setup():
        import jax, jax.numpy as jnp
        import numpy as np
        NEG_INF = -1000000000.0
        LEAKY_SLOPE = 0.2
        key = jax.random.key(seed)
        k1, k2, k3, k4 = jax.random.split(key, 4)
        N, F_in, F_out = (4096, 128, 128)
        h = jax.random.normal(k1, (N, F_in), dtype=jnp.float32)
        adj = jax.random.randint(k2, (N, N), 0, 2, dtype=jnp.int32)
        W = jax.random.normal(k3, (F_out, F_in), dtype=jnp.float32) / np.sqrt(F_in)
        a = jax.random.normal(k4, (2 * F_out,), dtype=jnp.float32) / np.sqrt(2 * F_out)
        return {'h': h, 'adj': adj, 'W': W, 'a': a}
    _L0_gnn_all = _L0_gnn_setup()
    _L0_gnn_in = {k: v for k, v in _L0_gnn_all.items() if k in ('W', 'a')}
    del _L0_gnn_all
    return {'x': x, 'adj': adj, 'L0_gnn_W': _L0_gnn_in['W'], 'L0_gnn_a': _L0_gnn_in['a']}

def reference(x, adj, L0_gnn_W, L0_gnn_a):
    import jax
    import jax.numpy as jnp

    def _L0_gnn_ref(h, adj, W, a):
        import jax, jax.numpy as jnp
        import numpy as np
        NEG_INF = -1000000000.0
        LEAKY_SLOPE = 0.2
        Wh = h @ W.T
        F_out = Wh.shape[1]
        a1, a2 = (a[:F_out], a[F_out:])
        s1 = Wh @ a1
        s2 = Wh @ a2
        e = jax.nn.leaky_relu(s1[:, None] + s2[None, :], negative_slope=LEAKY_SLOPE)
        e = jnp.where(adj == 0, NEG_INF, e)
        attention = jax.nn.softmax(e, axis=1)
        return attention @ Wh
    h = jnp.maximum(_layernorm(x, axis=-1), 0.0)
    x = x + _L0_gnn_ref(h, adj, L0_gnn_W, L0_gnn_a)
    return x

_drawn_inputs = setup_inputs


def setup_inputs(seed=0):
    import zlib

    import numpy as np

    out = dict(_drawn_inputs(seed))
    spreads = {}
    factors = {}
    for name, (base, spread) in spreads.items():
        noise = np.random.default_rng([zlib.crc32(name.encode()), seed]).standard_normal(out[name].shape)
        drawn = base * np.exp(spread * noise) if base else spread * noise
        out[name] = jnp.asarray(drawn.astype(out[name].dtype))
    for name, factor in factors.items():
        out[name] = (out[name] * factor).astype(out[name].dtype)
    return out
```

```python
from contextlib import ExitStack

import concourse.bass as bass
from concourse import mybir

ALU = mybir.AluOpType
ACT = mybir.ActivationFunctionType
F32 = mybir.dt.float32
F16 = mybir.dt.float16
BF16 = mybir.dt.bfloat16
I32 = mybir.dt.int32
U32 = mybir.dt.uint32
AX_X = mybir.AxisListType.X
RMAX = bass.bass_isa.ReduceOp.max

P = 128
SLOPE = 0.2
LN_EPS = 1e-5
STEP = 7.5
TAU = 2.0 ** 14 * 3.3546263e-4
TOP = 2.0 ** 14
TINY = 1e-30

XB = 3
XT = 8
NADJ = 4
ACOLS = 1024
GT = 2
ST = ACOLS // P
NB = 2


def build_gat(nc, x, adj, W, a, out):
    N, F = x.shape
    NT = N // P
    NX = NT // XT
    NG = NT // GT
    GR = GT * P
    NS = NT // ST
    CG = N // ACOLS
    F1 = F + 1
    SW = ST * GR
    LAG = 2
    VLAG = 3

    adj_v = adj.rearrange("(g t p) n -> g p t n", t=GT, p=P)
    x_v = x.rearrange("(c t p) f -> c p t f", t=XT, p=P)
    out_v = out.rearrange("(g t p) f -> g p t f", t=GT, p=P)

    with ExitStack() as ctx:
        def sb(name, shape, dt):
            return ctx.enter_context(nc.sbuf_tensor(name, shape, dt))

        def sem(name):
            return ctx.enter_context(nc.semaphore(name))

        adj_sb = [sb(f"adj_sb{i}", [P, GT, ACOLS], I32) for i in range(NADJ)]
        s2row = sb("s2row", [P, N], F32)
        wh = sb("wh", [P, NT, F + 2], F32)
        w16 = sb("w16", [P, NT, 2, 2, F1], F16)
        shared = sb("shared", [P, 7 * SW // 2 + 2 * XT * F1], F32)

        def floats(start, *shape):
            size = 1
            for k in shape:
                size *= k
            v = shared[:, start:start + size]
            return v if len(shape) == 1 else v.rearrange("p (t f) -> p t f", f=shape[1])

        def halves(n, dt):
            return shared[:, n * SW // 2:(n + 1) * SW // 2].bitcast(dt)

        XC = XT * F
        x_sb = [floats(i * XC, XT, F) for i in range(XB)]
        sq = [floats((XB + i) * XC, XT, F) for i in range(2)]
        hT = [floats((XB + 2 + i) * XC, XC) for i in range(2)]
        at = (XB + 4) * XC
        w_sb, wa2, hbar_rep, ones, wx = (floats(at + i * P, w) for i, w in enumerate((F, P, P, P, F + 2)))

        edge = [halves(n, BF16) for n in (0, 1)]
        posm = [halves(n, F16) for n in (2, 3)]
        negm = [halves(n, F16) for n in (4, 5)]
        sign = halves(6, BF16)
        at = 7 * SW // 2
        w32 = [floats(at + i * XT * F1, XT, F1) for i in range(2)]
        part = shared[:, at:at + 4 * GT * F1].rearrange("p (m t f) -> p m t f", m=2, t=GT)
        at += 4 * GT * F1
        quad = shared[:, at:at + 2 * GT * F1].rearrange("p (m t f) -> p m t f", m=2, t=GT)
        num = floats(at + 2 * GT * F1, GT, F1)
        res = floats(at + 3 * GT * F1, GT, F)
        old = sb("old", [P, GT, F], F32)
        ident = sb("ident", [P, P], F32)
        ident16 = sb("ident16", [P, P], BF16)
        a_sb = sb("a_sb", [P, 2], F32)
        hsum = sb("hsum", [P, NX], F32)
        hbar = sb("hbar", [P, 1], F32)
        mean = sb("mean", [P, F], F32)
        total = sb("total", [P, NT], F32)
        mu = sb("mu", [P, NT], F32)
        var = sb("var", [P, NT], F32)
        sd = sb("sd", [P, NT], F32)
        y = [sb(f"y{i}", [P, XT], F32) for i in range(4)]
        rstd = sb("rstd", [P, NT], F32)
        whmax = sb("whmax", [P, NX], F32)
        ns2 = sb("ns2", [P, NT], F32)
        peak = sb("peak", [P, 4], F32)
        top = sb("top", [P, 4], F32)
        span = sb("span", [P, 4], F32)
        s1odd = sb("s1odd", [P, NT], F32)
        cref = sb("cref", [P, 1], F32)
        whm = sb("whm", [P, 1], F32)
        rwhm = sb("rwhm", [P, 1], F32)
        tcol = sb("tcol", [P, NT], F32)
        ecol = sb("ecol", [P, 2, NT], F32)
        escale = sb("escale", [P, 2, NT], F32)
        eden = sb("eden", [P, 2, NT], F32)
        urow = sb("urow", [P, NT], F32)
        mrow = sb("mrow", [P, NT], F32)
        drow = sb("drow", [P, 2, NT], F32)
        ab = sb("ab", [P, 2, NT], F32)
        live = sb("live", [P, NT], F32)
        first = sb("first", [P, 1], F32)
        spread = [sb(f"spread{i}", [P, 1], F32) for i in range(4)]
        n_floor = sb("n_floor", [P, 1], I32)
        n_rounds = sb("n_rounds", [P, 1], I32)
        sel = sb("sel", [P, GT], F32)
        den = sb("den", [P, GT], F32)
        rden = sb("rden", [P, GT], F32)
        rs = sb("rs", [P, GT], F32)
        fm = sb("fm", [P, GT], F32)

        turned = [ctx.enter_context(nc.psum_tensor(f"turned{i}", [P, XT * P], F32)) for i in range(2)]
        turned16 = [v[:].bitcast(BF16) for v in turned]
        acc = ctx.enter_context(nc.psum_tensor("acc", [P, 2 * GT, 512], F32))

        x_in = [sem(f"x_in{i}") for i in range(XB)]
        adj_in = [sem(f"adj_in{i}") for i in range(NADJ)]
        w_in = sem("w_in")
        a_in = sem("a_in")
        out_is_x = sem("out_is_x")
        old_in = sem("old_in")
        out_stored = sem("out_stored")
        consts = sem("consts")
        dve_done = sem("dve_done")
        wx_psum = sem("wx_psum")
        wx_ready = sem("wx_ready")
        mu_ready = sem("mu_ready")
        xc_ready = sem("xc_ready")
        sq_ready = sem("sq_ready")
        var_ready = sem("var_ready")
        sd_ready = sem("sd_ready")
        h_ready = sem("h_ready")
        ht_psum = sem("ht_psum")
        ht_ready = sem("ht_ready")
        wh_psum = sem("wh_psum")
        wh_ready = sem("wh_ready")
        s2_ready = sem("s2_ready")
        hbar_ready = sem("hbar_ready")
        mean_psum = sem("mean_psum")
        peak_ready = sem("peak_ready")
        top_ready = sem("top_ready")
        texp_in = sem("texp_in")
        texp_out = sem("texp_out")
        w32_ready = sem("w32_ready")
        whigh_ready = sem("whigh_ready")
        wlow_ready = sem("wlow_ready")
        mean_ready = sem("mean_ready")
        rounds_known = sem("rounds_known")
        step_turned = sem("step_turned")
        step_out = sem("step_out")
        edge_ready = sem("edge_ready")
        masks_ready = sem("masks_ready")
        step_summed = sem("step_summed")
        pos_part = sem("pos_part")
        neg_part = sem("neg_part")
        quad_ready = sem("quad_ready")
        num_ready = sem("num_ready")
        fin_chain = sem("fin_chain")
        factors_ready = sem("factors_ready")
        pool_chain = sem("pool_chain")
        new_ready = sem("new_ready")

        block = ctx.enter_context(nc.Block())

        def wait(eng, semaphore, value):
            if not (isinstance(value, int) and value <= 0):
                eng.wait_ge(semaphore, value)

        def rounds(eng, one):
            one(0)
            eng.wait_ge(rounds_known, 1)
            n = eng.value_load(n_rounds[0:1, 0:1], min_val=1)
            with eng.If(n > 1):
                with eng.Fori(1, n) as r:
                    one(r)

        def groups(eng, r, group):
            group(r, 0, True)
            with eng.Fori(1, NG - 1) as g:
                group(r, g, True)
            group(r, NG - 1, False)

        @block.sync
        def _(sp):
            def load_x(c):
                if c >= XB:
                    sp.wait_ge(ht_psum, c - XB + 1)
                sp.dma_start(x_sb[c % XB], x_v[c]).then_inc(x_in[c % XB], 16)

            def load_adj(r, g, k):
                n = (r * NG + g) * CG + k
                wait(sp, edge_ready, n - NADJ + 1)
                sp.dma_start(adj_sb[k % NADJ][:], adj_v[g, :, :, k * ACOLS:(k + 1) * ACOLS])\
                  .then_inc(adj_in[k % NADJ], 16)

            sp.dma_start(w_sb, W).then_inc(w_in, 16)
            for c in range(XB):
                load_x(c)
            for c in range(XB, NX):
                if c - XB < NADJ:
                    load_adj(0, 0, c - XB)
                load_x(c)
            for k in range(NX - XB, NADJ):
                load_adj(0, 0, k)
            sp.dma_start(out.rearrange("(p r) f -> p (r f)", p=P), x.rearrange("(p r) f -> p (r f)", p=P))\
              .then_inc(out_is_x, 16)

            def one_round(r):
                for k in range(NADJ if isinstance(r, int) else 0, CG):
                    load_adj(r, 0, k)
                with sp.Fori(1, NG) as g:
                    for k in range(CG):
                        load_adj(r, g, k)

            rounds(sp, one_round)

        @block.gpsimd
        def _(pool):
            pool.dma_start(a_sb[:], a.rearrange("(k p) -> p k", p=P), allow_slow_non_contiguous=True).then_inc(a_in, 16)
            nc.gpsimd.memset(ident[:], 0.0).then_inc(consts, 1)
            nc.gpsimd.memset(ones, 1.0).then_inc(consts, 1)
            pool.wait_ge(consts, 2)
            nc.gpsimd.affine_select(out=ident[:], in_=ident[:], compare_op=ALU.not_equal, fill=1.0, base=0,
                                    pattern=[[-1, P]], channel_multiplier=1).then_inc(consts, 1)
            pool.wait_ge(consts, 3)
            nc.gpsimd.tensor_copy(ident16[:], ident[:]).then_inc(consts, 1)
            nc.gpsimd.memset(live[:], 1.0).then_inc(consts, 1)
            nc.gpsimd.memset(first[:], 1.0).then_inc(consts, 1)
            for c in range(NX):
                pool.wait_ge(mu_ready, c + 1)
                t = slice(c * XT, (c + 1) * XT)
                nc.gpsimd.tensor_tensor(x_sb[c % XB], x_sb[c % XB], mu[:, t].unsqueeze(2).to_broadcast([P, XT, F]),
                                        ALU.subtract).then_inc(xc_ready, 1)
            pool.wait_ge(peak_ready, 1)
            nc.gpsimd.partition_all_reduce(top[:], peak[:], P, RMAX).then_inc(top_ready, 1)

            def finish(r, g):
                q = r * NG + g
                pool.wait_ge(pos_part, q + 1)
                pool.wait_ge(neg_part, q + 1)
                nc.gpsimd.tensor_tensor(quad, part[:, :, :, 0:F1], part[:, :, :, F1:2 * F1],
                                        ALU.add).then_inc(quad_ready, 1)
                pool.wait_ge(quad_ready, q + 1)
                nc.gpsimd.tensor_tensor(num, quad[:, 0], quad[:, 1], ALU.add).then_inc(num_ready, 1)
                pool.wait_ge(factors_ready, q + 1)
                wait(pool, out_stored, 16 * q)
                nc.gpsimd.tensor_tensor(res, num[:, :, 0:F], rs[:].unsqueeze(2).to_broadcast([P, GT, F]),
                                        ALU.mult).then_inc(pool_chain, 1)
                fill = quad[:, 0, :, 0:F]
                nc.gpsimd.tensor_tensor(fill, mean[:].unsqueeze(1).to_broadcast([P, GT, F]),
                                        fm[:].unsqueeze(2).to_broadcast([P, GT, F]), ALU.mult).then_inc(pool_chain, 1)
                pool.wait_ge(pool_chain, 3 * q + 2)
                nc.gpsimd.tensor_tensor(res, res, fill, ALU.add).then_inc(pool_chain, 1)
                pool.wait_ge(pool_chain, 3 * q + 3)
                pool.wait_ge(old_in, 16 * (q + 1))
                nc.gpsimd.tensor_tensor(res, old[:], res, ALU.add).then_inc(new_ready, 1)

            def one_round(r):
                for j in range(2 * NX):
                    k, m = j // 2, j % 2
                    t = slice(k * XT, (k + 1) * XT)
                    pool.wait_ge(whigh_ready, r * 2 * NX + j + 1)
                    nc.gpsimd.tensor_tensor(w16[:, t, m, 1, :], w32[j % 2], w16[:, t, m, 0, :],
                                            ALU.subtract).then_inc(wlow_ready, 1)
                if isinstance(r, int):
                    pool.wait_ge(mean_ready, 1)
                finish(r, 0)
                with pool.Fori(1, NG) as g:
                    finish(r, g)

            rounds(pool, one_round)

        @block.scalar
        def _(act):
            def square(c):
                act.wait_ge(xc_ready, c + 1)
                nc.scalar.activation(sq[c % 2], x_sb[c % XB], ACT.Square).then_inc(sq_ready, 1)

            def wh_out(c):
                act.wait_ge(wh_psum, c + 1)
                v = acc[:, :, :].rearrange("p b (h w) -> p (b h) w", h=2)
                nc.scalar.activation(wh[:, c * XT:(c + 1) * XT, :], v[:, :, 0:F + 2], ACT.Copy).then_inc(wh_ready, 1)
                nc.scalar.activation(s2row[:, c * XT * P:(c + 1) * XT * P], turned[c % 2][:], ACT.Copy)\
                    .then_inc(s2_ready, 1)

            square(0)
            for c in range(NX):
                act.wait_ge(var_ready, c + 1)
                nc.scalar.activation(sd[:, c * XT:(c + 1) * XT], var[:, c * XT:(c + 1) * XT], ACT.Sqrt)\
                    .then_inc(sd_ready, 1)
                if c + 1 < NX:
                    square(c + 1)
                if c:
                    wh_out(c - 1)
                act.wait_ge(ht_psum, c + 1)
                nc.scalar.activation(hT[c % 2], turned[c % 2][:], ACT.Copy,
                                     accum_out=hsum[:, c:c + 1]).then_inc(ht_ready, 1)
            wh_out(NX - 1)

            def step(r, g, s):
                n = (r * NG + g) * NS + s
                act.wait_ge(step_turned, n + 1)
                wait(act, masks_ready, n)
                nc.scalar.activation(sign, turned16[s % NB], ACT.Sign)\
                    .then_inc(step_out, 1)

            def sums_out(r, g):
                act.wait_ge(step_summed, (r * NG + g + 1) * NS)
                for t in range(GT):
                    last = nc.scalar.activation(part[:, 0, t, :], acc[:, 2 * t, 0:2 * F1], ACT.Copy,
                                                scale=ab[:, 0, bass.ds(g * GT + t, 1)])
                last.then_inc(pos_part, 1)

            def load_old(g):
                act.dma_start(old[:], out_v[g]).then_inc(old_in, 16)

            def store(r, g):
                act.wait_ge(new_ready, r * NG + g + 1)
                act.dma_start(out_v[g], res).then_inc(out_stored, 16)

            def one_round(r):
                act.wait_ge(texp_in, 2 * r + 1)
                nc.scalar.activation(ecol[:, 0], tcol[:], ACT.Exp).then_inc(texp_out, 1)
                nc.scalar.activation(ecol[:, 1], tcol[:], ACT.Exp, scale=SLOPE).then_inc(texp_out, 1)
                act.wait_ge(texp_in, 2 * r + 2)
                nc.scalar.activation(ab[:], drow[:], ACT.Exp).then_inc(texp_out, 1)
                for j in range(2 * NX):
                    k, m = j // 2, j % 2
                    act.wait_ge(w32_ready, 2 * (r * 2 * NX + j + 1))
                    nc.scalar.activation(w16[:, k * XT:(k + 1) * XT, m, 0, :], w32[j % 2], ACT.Copy)\
                        .then_inc(whigh_ready, 1)
                if isinstance(r, int):
                    act.wait_ge(out_is_x, 16)
                for s in range(NS):
                    step(r, 0, s)
                with act.Fori(1, NG) as g:
                    for s in range(NS):
                        step(r, g, s)
                        if s == LAG - 1:
                            sums_out(r, g - 1)
                        if s == 2:
                            load_old(g - 1)
                        if s == 5:
                            store(r, g - 1)
                sums_out(r, NG - 1)
                load_old(NG - 1)
                store(r, NG - 1)
                act.wait_ge(out_stored, 16 * NG * (r + 1))

            rounds(act, one_round)

        @block.vector
        def _(dve):
            chain = [0]
            earlier = [0]

            def link(ins):
                chain[0] += 1
                ins.then_inc(dve_done, 1)
                dve.wait_ge(dve_done, earlier[0] + chain[0])

            dve.wait_ge(wx_psum, 2)
            link(nc.vector.tensor_copy(wx[:, 0:F], acc[:, 0, 0:F]))
            link(nc.vector.tensor_copy(wx[:, F:F + 2], acc[:, 1, 0:2]))
            dve.wait_ge(consts, 2)
            nc.vector.tensor_scalar(wa2, ones, wx[:, F + 1:F + 2], None, ALU.mult).then_inc(wx_ready, 1)

            def means(c):
                t = slice(c * XT, (c + 1) * XT)
                dve.wait_ge(x_in[c % XB], 16 * (c // XB + 1))
                link(nc.vector.tensor_reduce(total[:, t], x_sb[c % XB], AX_X, ALU.add))
                nc.vector.tensor_scalar(mu[:, t], total[:, t], 1.0 / F, None, ALU.mult).then_inc(mu_ready, 1)

            def highest_wh(c):
                dve.wait_ge(wh_ready, c + 1)
                nc.vector.tensor_reduce(whmax[:, c:c + 1], wh[:, c * XT:(c + 1) * XT, 0:F],
                                        mybir.AxisListType.XY, ALU.max, apply_absolute_value=True)\
                    .then_inc(dve_done, 1)
                chain[0] += 1

            means(0)
            for c in range(NX):
                t = slice(c * XT, (c + 1) * XT)
                dve.wait_ge(sq_ready, c + 1)
                link(nc.vector.tensor_reduce(total[:, t], sq[c % 2], AX_X, ALU.add))
                nc.vector.tensor_scalar(var[:, t], total[:, t], 1.0 / F, LN_EPS, ALU.mult, ALU.add)\
                    .then_inc(var_ready, 1)
                if c + 1 < NX:
                    means(c + 1)
                dve.wait_ge(sd_ready, c + 1)
                link(nc.vector.reciprocal(y[0][:], sd[:, t]))
                link(nc.vector.tensor_tensor(y[1][:], y[0][:], y[0][:], ALU.mult))
                link(nc.vector.tensor_tensor(y[2][:], y[1][:], var[:, t], ALU.mult))
                link(nc.vector.tensor_scalar(y[3][:], y[2][:], -0.5, 1.5, ALU.mult, ALU.add))
                link(nc.vector.tensor_tensor(rstd[:, t], y[0][:], y[3][:], ALU.mult))
                nc.vector.scalar_tensor_tensor(out=x_sb[c % XB], in0=x_sb[c % XB], scalar=0.0,
                                               in1=rstd[:, t].unsqueeze(2).to_broadcast([P, XT, F]),
                                               op0=ALU.max, op1=ALU.mult).then_inc(h_ready, 1)
                if c > 1:
                    highest_wh(c - 2)
            highest_wh(NX - 2)
            highest_wh(NX - 1)
            dve.wait_ge(dve_done, chain[0])
            s1, s2 = wh[:, :, F], wh[:, :, F + 1]
            link(nc.vector.tensor_scalar(ns2[:], s2, -1.0, None, ALU.mult))
            nc.vector.tensor_reduce(peak[:, 0:1], s2, AX_X, ALU.max)
            nc.vector.tensor_reduce(peak[:, 1:2], whmax[:], AX_X, ALU.max)
            nc.vector.tensor_reduce(peak[:, 2:3], ns2[:], AX_X, ALU.max)
            nc.vector.tensor_reduce(peak[:, 3:4], s1, AX_X, ALU.max, apply_absolute_value=True).then_inc(peak_ready, 1)
            dve.wait_ge(ht_ready, NX)
            link(nc.vector.tensor_reduce(hbar[:], hsum[:], AX_X, ALU.add))
            nc.vector.tensor_scalar(hbar_rep, ones, hbar[:], 1.0 / N, ALU.mult, ALU.mult).then_inc(hbar_ready, 1)

            dve.wait_ge(top_ready, 1)
            link(nc.vector.tensor_reduce(span[:, 0:1], top[:, 0:4:1], AX_X, ALU.max))
            link(nc.vector.tensor_scalar(span[:, 1:2].bitcast(I32), span[:, 0:1].bitcast(I32), 0x7F800000, None,
                                         ALU.bitwise_and))
            link(nc.vector.tensor_scalar(span[:, 2:3], span[:, 1:2], 12.0, None, ALU.mult))
            link(nc.vector.tensor_scalar(span[:, 3:4], span[:, 1:2], 2.0 ** -21, None, ALU.mult))
            link(nc.vector.tensor_scalar(s1odd[:], s1, span[:, 2:3], span[:, 2:3], ALU.add, ALU.subtract))
            link(nc.vector.tensor_scalar(s1odd[:], s1odd[:], span[:, 3:4], None, ALU.add))
            dve.wait_ge(s2_ready, NX)
            link(nc.vector.tensor_scalar(s2row[:], s2row[:], span[:, 2:3], span[:, 2:3], ALU.add, ALU.subtract))

            link(nc.vector.tensor_tensor(spread[0][:], top[:, 0:1], top[:, 2:3], ALU.add))
            link(nc.vector.tensor_scalar(spread[1][:], spread[0][:], 1.0 / STEP, None, ALU.mult))
            link(nc.vector.tensor_copy(n_floor[:], spread[1][:]))
            link(nc.vector.tensor_copy(spread[2][:], n_floor[:]))
            link(nc.vector.tensor_tensor(spread[3][:], spread[2][:], spread[1][:], ALU.is_lt))
            nc.vector.tensor_scalar(n_rounds[:], spread[2][:], spread[3][:], 1.0, ALU.add, ALU.max)\
                .then_inc(rounds_known, 1)

            def weights(r):
                if isinstance(r, int):
                    link(nc.vector.tensor_copy(cref[:], top[:, 0:1]))
                else:
                    dve.wait_ge(out_stored, 16 * NG * r)
                    dve.wait_ge(step_summed, NG * NS * r)
                    nc.vector.memset(first[:], 0.0)
                    link(nc.vector.tensor_scalar(cref[:], cref[:], -STEP, None, ALU.add))
                nc.vector.tensor_scalar(tcol[:], s2, cref[:], 0.0, ALU.subtract, ALU.min).then_inc(texp_in, 1)
                link(nc.vector.tensor_scalar(whm[:], top[:, 1:2], TINY, None, ALU.max))
                link(nc.vector.reciprocal(rwhm[:], whm[:]))
                link(nc.vector.tensor_scalar(urow[:], s1, cref[:], None, ALU.add))
                link(nc.vector.scalar_tensor_tensor(out=mrow[:], in0=urow[:], scalar=SLOPE, in1=urow[:],
                                                    op0=ALU.mult, op1=ALU.max))
                nc.vector.tensor_tensor(drow[:, 0], urow[:], mrow[:], ALU.subtract)
                nc.vector.scalar_tensor_tensor(out=drow[:, 1], in0=urow[:], scalar=SLOPE, in1=mrow[:],
                                               op0=ALU.mult, op1=ALU.subtract).then_inc(texp_in, 1)
                dve.wait_ge(texp_out, 3 * r + 2)
                link(nc.vector.tensor_scalar(escale[:], ecol[:], rwhm[:], TOP, ALU.mult, ALU.mult))
                link(nc.vector.tensor_scalar(eden[:], ecol[:], TOP, None, ALU.mult))
                if isinstance(r, int):
                    dve.wait_ge(mean_psum, 1)
                    nc.vector.tensor_copy(mean[:], acc[:, 3, 0:F]).then_inc(mean_ready, 1)
                    dve.wait_ge(s2_ready, NX)
                for j in range(2 * NX):
                    k, m = j // 2, j % 2
                    t = slice(k * XT, (k + 1) * XT)
                    wait(dve, wlow_ready, r * 2 * NX + j - 1)
                    nc.vector.tensor_tensor(w32[j % 2][:, :, 0:F], wh[:, t, 0:F],
                                            escale[:, m, t].unsqueeze(2).to_broadcast([P, XT, F]),
                                            ALU.mult).then_inc(w32_ready, 1)
                    nc.vector.tensor_copy(w32[j % 2][:, :, F], eden[:, m, t]).then_inc(w32_ready, 1)

            def edges(r, g, s):
                n = (r * NG + g) * NS + s
                dve.wait_ge(adj_in[s % NADJ], 16 * ((r * NG + g) * (CG // NADJ) + s // NADJ + 1))
                wait(dve, step_turned, n - NB + 1)
                for i in range(GT):
                    last = nc.vector.scalar_tensor_tensor(
                        out=edge[s % NB][:, i * ACOLS:(i + 1) * ACOLS], in0=s2row[:, s * ACOLS:(s + 1) * ACOLS],
                        scalar=s1odd[:, bass.ds(g * GT + i, 1)], in1=adj_sb[s % NADJ][:, i, :].bitcast(U32),
                        op0=ALU.add, op1=ALU.mult)
                last.then_inc(edge_ready, 1)

            def masks(r, g, s):
                n = (r * NG + g) * NS + s
                dve.wait_ge(step_out, n + 1)
                wait(dve, step_summed, n - NB + 1)
                nc.vector.tensor_scalar(posm[s % NB], sign, 0.0, None, ALU.max)
                nc.vector.tensor_scalar(negm[s % NB], sign, -1.0, 0.0, ALU.mult, ALU.max)\
                    .then_inc(masks_ready, 1)

            def sums_out(r, g):
                dve.wait_ge(step_summed, (r * NG + g + 1) * NS)
                for t in range(GT):
                    last = nc.vector.tensor_scalar(part[:, 1, t, :], acc[:, 2 * t + 1, 0:2 * F1],
                                                   ab[:, 1, bass.ds(g * GT + t, 1)], None, ALU.mult)
                last.then_inc(neg_part, 1)

            def factors(r, g):
                q = r * NG + g
                tiles = bass.ds(g * GT, GT)
                dve.wait_ge(num_ready, q + 1)
                nc.vector.scalar_tensor_tensor(out=sel[:], in0=num[:, :, F], scalar=TAU, in1=live[:, tiles],
                                               op0=ALU.is_ge, op1=ALU.mult).then_inc(fin_chain, 1)
                nc.vector.tensor_scalar(den[:], num[:, :, F], TINY, None, ALU.max).then_inc(fin_chain, 1)
                dve.wait_ge(fin_chain, 4 * q + 2)
                nc.vector.reciprocal(rden[:], den[:]).then_inc(fin_chain, 1)
                nc.vector.tensor_tensor(live[:, tiles], live[:, tiles], sel[:], ALU.subtract).then_inc(fin_chain, 1)
                dve.wait_ge(fin_chain, 4 * q + 4)
                nc.vector.scalar_tensor_tensor(out=rs[:], in0=rden[:], scalar=whm[:], in1=sel[:],
                                               op0=ALU.mult, op1=ALU.mult)
                nc.vector.tensor_scalar(fm[:], sel[:], -1.0, first[:], ALU.mult, ALU.add).then_inc(factors_ready, 1)

            def group(r, g, more):
                for s in range(NS):
                    masks(r, g, s)
                    if s + VLAG < NS:
                        edges(r, g, s + VLAG)
                    elif more:
                        edges(r, g + 1, s + VLAG - NS)
                    if not (isinstance(g, int) and g == 0):
                        if s == 0:
                            sums_out(r, g - 1)
                        if s == 2:
                            factors(r, g - 1)

            per_round = []

            def one_round(r):
                before = chain[0]
                if not isinstance(r, int):
                    earlier[0] = (r - 1) * per_round[0]
                weights(r)
                per_round.append(chain[0] - before)
                if isinstance(r, int):
                    dve.wait_ge(consts, 6)
                dve.wait_ge(texp_out, 3 * r + 3)
                for s in range(VLAG):
                    edges(r, 0, s)
                groups(dve, r, group)
                sums_out(r, NG - 1)
                factors(r, NG - 1)

            rounds(dve, one_round)
            assert per_round[0] == per_round[1]

        @block.tensor
        def _(pe):
            pe.wait_ge(consts, 3)
            pe.wait_ge(w_in, 16)
            pe.wait_ge(a_in, 16)
            nc.tensor.transpose(acc[:, 0, 0:F], w_sb, ident[:]).then_inc(wx_psum, 1)
            nc.tensor.matmul(acc[:, 1, 0:2], w_sb, a_sb[:], start=True, stop=True).then_inc(wx_psum, 1)
            pe.wait_ge(wx_ready, 1)

            def project(c):
                pe.wait_ge(ht_ready, c + 1)
                wait(pe, wh_ready, c)
                for i in range(XT):
                    o = (i % 2) * 256
                    nc.tensor.matmul(acc[:, i // 2, o:o + F + 2], hT[c % 2][:, i * P:(i + 1) * P], wx,
                                     start=True, stop=True)
                for q in range(XT * P // 512):
                    last = nc.tensor.matmul(turned[c % 2][:, q * 512:(q + 1) * 512], wa2,
                                            hT[c % 2][:, q * 512:(q + 1) * 512], start=True, stop=True)
                last.then_inc(wh_psum, 1)

            for c in range(NX):
                pe.wait_ge(h_ready, c + 1)
                wait(pe, s2_ready, c - 1)
                for i in range(XT):
                    last = nc.tensor.transpose(turned[c % 2][:, i * P:(i + 1) * P], x_sb[c % XB][:, i, :], ident[:])
                last.then_inc(ht_psum, 1)
                if c:
                    project(c - 1)
            project(NX - 1)
            pe.wait_ge(hbar_ready, 1)
            pe.wait_ge(wh_ready, NX)
            nc.tensor.matmul(acc[:, 3, 0:F], hbar_rep, wx[:, 0:F], start=True, stop=True).then_inc(mean_psum, 1)
            pe.wait_ge(s2_ready, NX)
            pe.wait_ge(consts, 4)
            pe.wait_ge(mean_ready, 1)

            def turn(r, g, s):
                n = (r * NG + g) * NS + s
                pe.wait_ge(edge_ready, n + 1)
                wait(pe, step_out, n - NB + 1)
                for t in range(ST):
                    for i in range(GT):
                        o = (t * GT + i) * P
                        last = nc.tensor.transpose(turned16[s % NB][:, o:o + P],
                                                   edge[s % NB][:, i * ACOLS + t * P:i * ACOLS + (t + 1) * P],
                                                   ident16[:])
                last.then_inc(step_turned, 1)

            def products(r, g, s):
                n = (r * NG + g) * NS + s
                b = s % NB
                if s == 0:
                    wait(pe, pos_part, r * NG + g)
                    wait(pe, neg_part, r * NG + g)
                if isinstance(g, int) and g == 0:
                    pe.wait_ge(wlow_ready, r * 2 * NX + 2 * (s * ST // XT + 1))
                pe.wait_ge(masks_ready, n + 1)
                for t in range(ST):
                    for i in range(GT):
                        for m, mask in enumerate((posm, negm)):
                            o = t * GR + i * P
                            last = nc.tensor.matmul(acc[:, 2 * i + m, 0:2 * F1], mask[b][:, o:o + P],
                                                    w16[:, s * ST + t, m, :, :],
                                                    start=(s == 0 and t == 0), stop=(s == NS - 1 and t == ST - 1))
                last.then_inc(step_summed, 1)

            def group(r, g, more):
                for s in range(NS):
                    if s + LAG < NS:
                        turn(r, g, s + LAG)
                    elif more:
                        turn(r, g + 1, s + LAG - NS)
                    products(r, g, s)

            def one_round(r):
                for s in range(LAG):
                    turn(r, 0, s)
                groups(pe, r, group)

            rounds(pe, one_round)


_INS = ['x', 'adj', 'L0_gnn_W', 'L0_gnn_a']


def kernel(**inputs):
    import numpy as _np
    import concourse.bacc as _bacc
    from concourse import mybir as _mybir
    from concourse.bass_utils import run_bass_kernel_spmd as _run

    nc = _bacc.Bacc("TRN2", target_bir_lowering=False, num_devices=1)
    arrays, args = {}, []
    for name in _INS:
        v = _np.ascontiguousarray(inputs[name])
        arrays[f"in_{name}_dram"] = v
        args.append(nc.dram_tensor(f"in_{name}_dram", v.shape, _mybir.dt.from_np(v.dtype), kind="ExternalInput").ap())
    out = nc.dram_tensor("out_0_dram", inputs['x'].shape, _mybir.dt.float32, kind="ExternalOutput").ap()
    build_gat(nc, *args, out)
    r = _run(nc, [arrays], core_ids=[0])
    return r.results[0]["out_0_dram"]
```

```python
from contextlib import ExitStack

import concourse.bass as bass
from concourse import mybir

ALU = mybir.AluOpType
ACT = mybir.ActivationFunctionType
F32 = mybir.dt.float32
F16 = mybir.dt.float16
BF16 = mybir.dt.bfloat16
F8 = mybir.dt.float8e5
I32 = mybir.dt.int32
U32 = mybir.dt.uint32
AX_X = mybir.AxisListType.X
RMAX = bass.bass_isa.ReduceOp.max

P = 128
SLOPE = 0.2
LN_EPS = 1e-5
STEP = 7.5
TAU = 2.0 ** 14 * 3.3546263e-4
TOP = 2.0 ** 14
TINY = 1e-20

XT = 8
NADJ = 4
ACOLS = 1024
GT = 2
ST = ACOLS // P
NB = 2
NE = 4
GRID = 1536.0
HALF = 2.0 ** -14


def build_gat(nc, x, adj, W, a, out):
    N, F = x.shape
    NT = N // P
    NX = NT // XT
    NG = NT // GT
    GR = GT * P
    NS = NT // ST
    CG = N // ACOLS
    F1 = F + 1
    SW = ST * GR
    BATCHES = [(0, 1)] + [(c, min(c + 2, NX)) for c in range(1, NX, 2)]
    LAG = 2
    VLAG = 3

    assert GT == 2
    adj_v = adj.rearrange("(g p t) n -> g p t n", t=GT, p=P)
    x_v = x.rearrange("(c g p t) f -> c p g t f", g=XT // GT, t=GT, p=P)
    x_g = x.rearrange("(g p t) f -> g p t f", t=GT, p=P)
    out_v = out.rearrange("(g p t) f -> g p t f", t=GT, p=P)

    with ExitStack() as ctx:
        def sb(name, shape, dt):
            return ctx.enter_context(nc.sbuf_tensor(name, shape, dt))

        def sem(name):
            return ctx.enter_context(nc.semaphore(name))

        adj_sb = [sb(f"adj_sb{i}", [P, GT, ACOLS], I32) for i in range(NADJ)]
        s2row = sb("s2row", [P, N], F32)
        wh = sb("wh", [P, NT, F + 2], F32)
        w16_bytes = sb("w16", [P, NT * 2 * 2 * F1], F16)
        w16 = w16_bytes[:].rearrange("p (t m k f) -> p t m k f", m=2, k=2, f=F1)
        first_stage = w16_bytes[:].bitcast(F32)
        x_sb = first_stage[:, 0:NT * F].rearrange("p (t f) -> p t f", f=F)
        at = NT * F
        w_sb, wsq, ones, wx = (first_stage[:, at + i * P:at + i * P + w] for i, w in enumerate((F, F, P, F + 2)))
        at += 3 * P + F + 2
        wh_sum = [first_stage[:, at + i * XT * F:at + (i + 1) * XT * F].rearrange("p (t f) -> p t f", f=F)
                  for i in range(2)]
        shared = sb("shared", [P, 7 * SW // 2 + 2 * XT * F1], F32)

        def floats(start, *shape):
            size = 1
            for k in shape:
                size *= k
            v = shared[:, start:start + size]
            return v if len(shape) == 1 else v.rearrange("p (t f) -> p t f", f=shape[1])

        def halves(n, dt):
            return shared[:, n * SW // 2:(n + 1) * SW // 2].bitcast(dt)

        XC = XT * F
        at = SW
        sq = [floats(at + i * XC, XT, F) for i in range(2)]
        hT = [floats(at + (2 + i) * XC, XC) for i in range(2)]

        edge = [shared[:, n * SW // NE:(n + 1) * SW // NE].bitcast(F8) for n in range(NE)]
        pairs = [shared[:, n * SW // NE:(n + 1) * SW // NE].bitcast(BF16) for n in range(NE)]
        posm = [halves(n, F16) for n in (2, 3)]
        negm = [halves(n, F16) for n in (4, 5)]
        sign = halves(6, BF16)
        at = 7 * SW // 2
        w32 = [floats(at + i * XT * F1, XT, F1) for i in range(2)]
        part = shared[:, at:at + 4 * GT * F1].rearrange("p (m t f) -> p m t f", m=2, t=GT)
        at += 4 * GT * F1
        quad = shared[:, at:at + 2 * GT * F1].rearrange("p (m t f) -> p m t f", m=2, t=GT)
        num = floats(at + 2 * GT * F1, GT, F1)
        res = floats(at + 3 * GT * F1, GT, F)
        old = sb("old", [P, GT, F], F32)
        ident = sb("ident", [P, P], F32)
        ident16 = sb("ident16", [P, P], BF16)
        a_sb = sb("a_sb", [P, 2], F32)
        mean = sb("mean", [P, F], F32)
        total = sb("total", [P, NT], F32)
        total_sq = sb("total_sq", [P, NT], F32)
        mu = sb("mu", [P, NT], F32)
        var = sb("var", [P, NT], F32)
        sd = sb("sd", [P, NT], F32)
        y = [sb(f"y{i}", [P, 2 * XT], F32) for i in range(3)]
        rstd = sb("rstd", [P, NT], F32)
        ns2 = sb("ns2", [P, NT], F32)
        peak = sb("peak", [P, 2], F32)
        top = sb("top", [P, 2], F32)
        wasq = sb("wasq", [P, 2], F32)
        rowsq = sb("rowsq", [P, 1], F32)
        norms = sb("norms", [P, 3], F32)
        bound = sb("bound", [P, 3], F32)
        span = sb("span", [P, 4], F32)
        off_grid = sb("off_grid", [P, NT, 2], F32)
        on_grid = sb("on_grid", [P, NT], F32)
        s1odd = sb("s1odd", [P, NT], F32)
        s1_now = sb("s1_now", [P, GT], F32)
        cref = sb("cref", [P, 1], F32)
        whm = sb("whm", [P, 1], F32)
        rwhm = sb("rwhm", [P, 1], F32)
        tcol = sb("tcol", [P, NT], F32)
        ecol = sb("ecol", [P, 2, NT], F32)
        escale = sb("escale", [P, 2, NT], F32)
        eden = sb("eden", [P, 2, NT], F32)
        urow = sb("urow", [P, NT], F32)
        mrow = sb("mrow", [P, NT], F32)
        drow = sb("drow", [P, 2, NT], F32)
        ab = sb("ab", [P, 2, NT], F32)
        live = sb("live", [P, NT], F32)
        first = sb("first", [P, 1], F32)
        spread = [sb(f"spread{i}", [P, 1], F32) for i in range(4)]
        n_floor = sb("n_floor", [P, 1], I32)
        n_rounds = sb("n_rounds", [P, 1], I32)
        sel = sb("sel", [P, GT], F32)
        den = sb("den", [P, GT], F32)
        rden = sb("rden", [P, GT], F32)
        rs = sb("rs", [P, GT], F32)
        fm = sb("fm", [P, GT], F32)
        act_carrier = sb("act_carrier", [P, NS], F32)
        dve_carrier = sb("dve_carrier", [P, NS], F32)

        turned = [ctx.enter_context(nc.psum_tensor(f"turned{i}", [P, XT * P], F32)) for i in range(2)]
        turned16 = [turned[n // 2][:, n % 2 * 512:(n % 2 + 1) * 512].bitcast(BF16) for n in range(NE)]
        turned8 = [turned[n // 2][:, n % 2 * 512:(n % 2 + 1) * 512].bitcast(F8) for n in range(NE)]
        acc = ctx.enter_context(nc.psum_tensor("acc", [P, 2 * GT, 512], F32))
        acc_tiles = acc[:, :, :].rearrange("p b (h w) -> p (b h) w", h=2)

        x_in = [sem(f"x_in{i}") for i in range(NX)]
        adj_in = [sem(f"adj_in{i}") for i in range(NADJ)]
        w_in = sem("w_in")
        a_in = sem("a_in")
        old_in = sem("old_in")
        out_stored = sem("out_stored")
        consts = sem("consts")
        dve_done = sem("dve_done")
        wx_psum = sem("wx_psum")
        wx_ready = sem("wx_ready")
        rowsq_ready = sem("rowsq_ready")
        wasq_ready = sem("wasq_ready")
        wasq_psum = sem("wasq_psum")
        rowtop_ready = sem("rowtop_ready")
        norms_ready = sem("norms_ready")
        bound_ready = sem("bound_ready")
        mu_ready = sem("mu_ready")
        xc_ready = sem("xc_ready")
        sq_ready = sem("sq_ready")
        var_ready = sem("var_ready")
        sd_ready = sem("sd_ready")
        rstd_ready = sem("rstd_ready")
        ht_psum = sem("ht_psum")
        ht_ready = sem("ht_ready")
        wh_psum = sem("wh_psum")
        wh_ready = sem("wh_ready")
        grid_ready = sem("grid_ready")
        s1_ready = sem("s1_ready")
        s1_moved = sem("s1_moved")
        s2_psum = sem("s2_psum")
        s2_ready = sem("s2_ready")
        wh_added = sem("wh_added")
        mean_psum = sem("mean_psum")
        peak_ready = sem("peak_ready")
        top_ready = sem("top_ready")
        texp_in = sem("texp_in")
        texp_out = sem("texp_out")
        w32_ready = sem("w32_ready")
        whigh_ready = sem("whigh_ready")
        wlow_ready = sem("wlow_ready")
        mean_ready = sem("mean_ready")
        rounds_known = sem("rounds_known")
        step_turned = sem("step_turned")
        step_out = sem("step_out")
        edge_ready = sem("edge_ready")
        masks_ready = sem("masks_ready")
        neg_ready = sem("neg_ready")
        step_summed = sem("step_summed")
        tile_summed = [sem(f"tile_summed{i}") for i in range(GT - 1)]
        pos_part = sem("pos_part")
        neg_part = sem("neg_part")
        quad_ready = sem("quad_ready")
        num_ready = sem("num_ready")
        fin_chain = sem("fin_chain")
        factors_ready = sem("factors_ready")
        pool_chain = sem("pool_chain")
        new_ready = sem("new_ready")

        block = ctx.enter_context(nc.Block())

        def wait(eng, semaphore, value):
            if not (isinstance(value, int) and value <= 0):
                eng.wait_ge(semaphore, value)

        def wait_tile_summed(eng, r, g, t):
            if t < GT - 1:
                eng.wait_ge(tile_summed[t], r * NG + g + 1)
            else:
                eng.wait_ge(step_summed, (r * NG + g + 1) * NS)

        def rounds(eng, one):
            one(0)
            eng.wait_ge(rounds_known, 1)
            n = eng.value_load(n_rounds[0:1, 0:1], min_val=1)
            with eng.If(n > 1):
                with eng.Fori(1, n) as r:
                    one(r)

        def groups(eng, r, group):
            group(r, 0, True)
            with eng.Fori(1, NG - 1) as g:
                group(r, g, True)
            group(r, NG - 1, False)

        @block.sync
        def _(sp):
            def load_adj(r, g, k):
                n = (r * NG + g) * CG + k
                wait(sp, edge_ready, n - NADJ + 1)
                sp.dma_start(adj_sb[k % NADJ][:], adj_v[g, :, :, k * ACOLS:(k + 1) * ACOLS])\
                  .then_inc(adj_in[k % NADJ], 16)

            sp.dma_start(w_sb, W).then_inc(w_in, 16)
            for c in range(NX):
                sp.dma_start(x_sb[:, c * XT:(c + 1) * XT, :].rearrange("p (g t) f -> p g t f", t=GT), x_v[c]).then_inc(x_in[c], 16)
            for k in range(NADJ):
                load_adj(0, 0, k)

            def one_round(r):
                for k in range(NADJ if isinstance(r, int) else 0, CG):
                    load_adj(r, 0, k)
                with sp.Fori(1, NG) as g:
                    for k in range(CG):
                        load_adj(r, g, k)

            rounds(sp, one_round)

        @block.gpsimd
        def _(pool):
            pool.dma_start(a_sb[:], a.rearrange("(k p) -> p k", p=P), allow_slow_non_contiguous=True).then_inc(a_in, 16)
            nc.gpsimd.memset(ident[:], 0.0).then_inc(consts, 1)
            nc.gpsimd.memset(ones, 1.0).then_inc(consts, 1)
            pool.wait_ge(consts, 2)
            nc.gpsimd.affine_select(out=ident[:], in_=ident[:], compare_op=ALU.not_equal, fill=1.0, base=0,
                                    pattern=[[-1, P]], channel_multiplier=1).then_inc(consts, 1)
            pool.wait_ge(consts, 3)
            nc.gpsimd.tensor_copy(ident16[:], ident[:]).then_inc(consts, 1)
            nc.gpsimd.memset(live[:], 1.0).then_inc(consts, 1)
            nc.gpsimd.memset(first[:], 1.0).then_inc(consts, 1)
            pool.wait_ge(rowsq_ready, 1)
            nc.gpsimd.partition_all_reduce(norms[:, 2:3], rowsq[:], P, RMAX).then_inc(rowtop_ready, 1)

            def center(c):
                t = slice(c * XT, (c + 1) * XT)
                pool.wait_ge(mu_ready, c + 1)
                nc.gpsimd.tensor_tensor(x_sb[:, t, :], x_sb[:, t, :], mu[:, t].unsqueeze(2).to_broadcast([P, XT, F]),
                                        ALU.subtract).then_inc(xc_ready, 1)

            def add_wh(c):
                pool.wait_ge(wh_ready, c + 1)
                before = wh[:, 0:XT, 0:F] if c == 1 else wh_sum[c % 2]
                wait(pool, wh_added, c - 1)
                nc.gpsimd.tensor_tensor(wh_sum[(c + 1) % 2], before, wh[:, c * XT:(c + 1) * XT, 0:F],
                                        ALU.add).then_inc(wh_added, 1)

            for c in range(NX):
                center(c)
                if c > 3:
                    add_wh(c - 3)
            for c in range(NX - 3, NX - 1):
                add_wh(c)
            pool.wait_ge(peak_ready, 1)
            nc.gpsimd.partition_all_reduce(top[:], peak[:], P, RMAX).then_inc(top_ready, 1)
            add_wh(NX - 1)

            def finish(r, g):
                q = r * NG + g
                pool.wait_ge(pos_part, GT * (q + 1))
                pool.wait_ge(neg_part, GT * (q + 1))
                nc.gpsimd.tensor_tensor(quad, part[:, :, :, 0:F1], part[:, :, :, F1:2 * F1],
                                        ALU.add).then_inc(quad_ready, 1)
                pool.wait_ge(quad_ready, q + 1)
                nc.gpsimd.tensor_tensor(num, quad[:, 0], quad[:, 1], ALU.add).then_inc(num_ready, 1)
                pool.wait_ge(factors_ready, q + 1)
                wait(pool, out_stored, 16 * q)
                nc.gpsimd.tensor_tensor(res, num[:, :, 0:F], rs[:].unsqueeze(2).to_broadcast([P, GT, F]),
                                        ALU.mult).then_inc(pool_chain, 1)
                fill = quad[:, 0, :, 0:F]
                nc.gpsimd.tensor_tensor(fill, mean[:].unsqueeze(1).to_broadcast([P, GT, F]),
                                        fm[:].unsqueeze(2).to_broadcast([P, GT, F]), ALU.mult).then_inc(pool_chain, 1)
                pool.wait_ge(pool_chain, 3 * q + 2)
                nc.gpsimd.tensor_tensor(res, res, fill, ALU.add).then_inc(pool_chain, 1)
                pool.wait_ge(pool_chain, 3 * q + 3)
                pool.wait_ge(old_in, 16 * (q + 1))
                nc.gpsimd.tensor_tensor(res, old[:], res, ALU.add).then_inc(new_ready, 1)

            def one_round(r):
                for j in range(2 * NX):
                    k, m = j // 2, j % 2
                    t = slice(k * XT, (k + 1) * XT)
                    pool.wait_ge(whigh_ready, r * 2 * NX + j + 1)
                    nc.gpsimd.tensor_tensor(w16[:, t, m, 1, :], w32[j % 2], w16[:, t, m, 0, :],
                                            ALU.subtract).then_inc(wlow_ready, 1)
                if isinstance(r, int):
                    pool.wait_ge(mean_ready, 1)
                finish(r, 0)
                with pool.Fori(1, NG) as g:
                    finish(r, g)

            rounds(pool, one_round)

        @block.scalar
        def _(act):
            def square(c):
                act.wait_ge(xc_ready, c + 1)
                wait(act, sq_ready, XT * (c - 1))
                for i in range(XT):
                    t = c * XT + i
                    nc.scalar.activation(sq[c % 2][:, i, :], x_sb[:, t, :], ACT.Square, accum_out=total_sq[:, t:t + 1])\
                        .then_inc(sq_ready, 1)

            def s2_out(c):
                act.wait_ge(s2_psum, c + 1)
                v = s2row[:, c * XT * P:(c + 1) * XT * P]
                nc.scalar.activation(v.rearrange("q (g p t) -> q g t p", t=GT, p=P),
                                     turned[c % 2][:].rearrange("q (g t p) -> q g t p", t=GT, p=P), ACT.Copy)\
                    .then_inc(s2_ready, 1)

            act.wait_ge(norms_ready, 1)
            act.wait_ge(rowtop_ready, 1)
            nc.scalar.activation(bound[:], norms[:], ACT.Sqrt, scale=1.01 * F).then_inc(bound_ready, 1)

            def root(c, end):
                act.wait_ge(var_ready, BATCHES.index((c, end)) + 1)
                nc.scalar.activation(sd[:, c * XT:end * XT], var[:, c * XT:end * XT], ACT.Sqrt).then_inc(sd_ready, 1)

            def relu_out(c):
                act.wait_ge(ht_psum, c + 1)
                wait(act, wh_psum, c - 1)
                nc.scalar.activation(hT[c % 2], turned[c % 2][:], ACT.Relu).then_inc(ht_ready, 1)

            square(0)
            root(*BATCHES[0])
            square(1)
            for c in range(NX):
                relu_out(c)
                if c:
                    for batch in BATCHES:
                        if batch[0] == c:
                            root(*batch)
                    s2_out(c - 1)
                if c + 2 < NX:
                    square(c + 2)
            s2_out(NX - 1)

            def step(r, g, s):
                n = (r * NG + g) * NS + s
                act.wait_ge(step_turned, n + 1)
                wait(act, masks_ready, n)
                nc.scalar.activation(act_carrier[:, s:s + 1], ident[:, 0:1], ACT.Copy)
                nc.scalar.activation(sign.rearrange("q (b k i) -> q b k i", k=2, i=P),
                                     turned8[s % NE].rearrange("q (b i k) -> q b k i", k=2, i=P), ACT.Sign)\
                    .then_inc(step_out, 1)
                if isinstance(g, int) and g == 0:
                    act.wait_ge(step_out, n + 1)
                    wait(act, step_summed, n - NB + 1)
                    nc.scalar.activation(negm[s % NB], sign, ACT.Relu, scale=-1.0).then_inc(neg_ready, 1)
                    act.wait_ge(neg_ready, r * NS + s + 1)

            def sums_out(r, g):
                for t in range(GT):
                    wait_tile_summed(act, r, g, t)
                    nc.scalar.activation(part[:, 0, t, :], acc[:, 2 * t, 0:2 * F1], ACT.Copy,
                                         scale=ab[:, 0, bass.ds(g * GT + t, 1)]).then_inc(pos_part, 1)

            def load_old(r, g):
                source = x_g if isinstance(r, int) else out_v
                act.dma_start(old[:], source[g]).then_inc(old_in, 16)

            def store(r, g):
                act.wait_ge(new_ready, r * NG + g + 1)
                act.dma_start(out_v[g], res).then_inc(out_stored, 16)

            def one_round(r):
                act.wait_ge(texp_in, 2 * r + 1)
                nc.scalar.activation(ecol[:, 0], tcol[:], ACT.Exp).then_inc(texp_out, 1)
                nc.scalar.activation(ecol[:, 1], tcol[:], ACT.Exp, scale=SLOPE).then_inc(texp_out, 1)
                act.wait_ge(texp_in, 2 * r + 2)
                nc.scalar.activation(ab[:], drow[:], ACT.Exp).then_inc(texp_out, 1)
                for s in range(NS):
                    for m in range(2):
                        j = 2 * s + m
                        act.wait_ge(w32_ready, 2 * (r * 2 * NX + j + 1))
                        nc.scalar.activation(w16[:, s * XT:(s + 1) * XT, m, 0, :], w32[m], ACT.Copy)\
                            .then_inc(whigh_ready, 1)
                    step(r, 0, s)
                with act.Fori(1, NG) as g:
                    for s in range(NS):
                        step(r, g, s)
                        if s == LAG - 1:
                            sums_out(r, g - 1)
                        if s == 2:
                            load_old(r, g - 1)
                        if s == 5:
                            store(r, g - 1)
                sums_out(r, NG - 1)
                load_old(r, NG - 1)
                store(r, NG - 1)
                act.wait_ge(out_stored, 16 * NG * (r + 1))

            rounds(act, one_round)

        @block.vector
        def _(dve):
            chain = [0]
            earlier = [0]

            def link(ins):
                chain[0] += 1
                ins.then_inc(dve_done, 1)
                dve.wait_ge(dve_done, earlier[0] + chain[0])

            def means(c):
                t = slice(c * XT, (c + 1) * XT)
                dve.wait_ge(x_in[c], 16)
                link(nc.vector.tensor_reduce(total[:, t], x_sb[:, t, :], AX_X, ALU.add))
                nc.vector.tensor_scalar(mu[:, t], total[:, t], 1.0 / F, None, ALU.mult).then_inc(mu_ready, 1)

            def variances(c, end):
                t = slice(c * XT, end * XT)
                dve.wait_ge(sq_ready, XT * end)
                nc.vector.tensor_scalar(var[:, t], total_sq[:, t], 1.0 / F, LN_EPS, ALU.mult, ALU.add)\
                    .then_inc(var_ready, 1)

            def deviations(c, end):
                t = slice(c * XT, end * XT)
                w = slice(0, (end - c) * XT)
                dve.wait_ge(sd_ready, BATCHES.index((c, end)) + 1)
                link(nc.vector.reciprocal(y[0][:, w], sd[:, t]))
                link(nc.vector.scalar_tensor_tensor(out=y[1][:, w], in0=y[0][:, w], scalar=-0.5, in1=y[0][:, w],
                                                    op0=ALU.mult, op1=ALU.mult))
                link(nc.vector.tensor_tensor(y[2][:, w], y[1][:, w], var[:, t], ALU.mult))
                link(nc.vector.scalar_tensor_tensor(out=rstd[:, t], in0=y[2][:, w], scalar=1.5, in1=y[0][:, w],
                                                    op0=ALU.add, op1=ALU.mult))

            def wh_out(c):
                t = slice(c * XT, (c + 1) * XT)
                dve.wait_ge(wh_psum, c + 1)
                nc.vector.tensor_tensor(wh[:, t, :], acc_tiles[:, :, 0:F + 2],
                                        rstd[:, t].unsqueeze(2).to_broadcast([P, XT, F + 2]), ALU.mult)\
                    .then_inc(wh_ready, 1)

            def to_grid(c):
                t = slice(c * XT, (c + 1) * XT)
                dve.wait_ge(wh_ready, c + 1)
                link(nc.vector.tensor_scalar(off_grid[:, t, :], wh[:, t, F:F + 2], span[:, 3:4], GRID, ALU.mult, ALU.add))
                nc.vector.tensor_scalar(on_grid[:, t], off_grid[:, t, 1], GRID, None, ALU.subtract)\
                    .then_inc(grid_ready, 1)
                nc.vector.tensor_scalar(s1odd[:, t], off_grid[:, t, 0], GRID, HALF, ALU.subtract, ALU.add)\
                    .then_inc(s1_ready, 1)

            def edges(r, g, s):
                n = (r * NG + g) * NS + s
                if s == 0:
                    wait(dve, edge_ready, n)
                    nc.vector.tensor_scalar(s1_now[:], s1odd[:, bass.ds(g * GT, GT)], 1.0, None, ALU.mult)\
                        .then_inc(s1_moved, 1)
                if s == 0:
                    dve.wait_ge(s1_moved, r * NG + g + 1)
                if isinstance(r, int) and isinstance(g, int) and g == 0:
                    dve.wait_ge(s2_ready, s + 1)
                dve.wait_ge(adj_in[s % NADJ], 16 * ((r * NG + g) * (CG // NADJ) + s // NADJ + 1))
                wait(dve, step_turned, n - NE + 1)
                nc.vector.memset(dve_carrier[:, s:s + 1], 0.0)
                for i in range(GT):
                    last = nc.vector.scalar_tensor_tensor(
                        out=edge[s % NE][:, i * ACOLS:(i + 1) * ACOLS], in0=s2row[:, s * ACOLS:(s + 1) * ACOLS],
                        scalar=s1_now[:, i:i + 1], in1=adj_sb[s % NADJ][:, i, :].bitcast(U32),
                        op0=ALU.add, op1=ALU.mult, saturate=False)
                last.then_inc(edge_ready, 1)

            means(0)
            means(1)
            dve.wait_ge(w_in, 16)
            link(nc.vector.tensor_tensor(wsq, w_sb, w_sb, ALU.mult))
            nc.vector.tensor_reduce(rowsq[:], wsq, AX_X, ALU.add).then_inc(rowsq_ready, 1)
            dve.wait_ge(wx_psum, 2)
            link(nc.vector.tensor_copy(wx[:, 0:F], acc[:, 0, 0:F]))
            nc.vector.tensor_copy(wx[:, F:F + 2], acc[:, 1, 0:2]).then_inc(wx_ready, 1)
            dve.wait_ge(wx_ready, 1)
            nc.vector.tensor_tensor(wasq[:], wx[:, F:F + 2], wx[:, F:F + 2], ALU.mult).then_inc(wasq_ready, 1)
            dve.wait_ge(wasq_psum, 1)
            nc.vector.tensor_copy(norms[:, 0:2], acc[:, 2, 0:2]).then_inc(norms_ready, 1)
            dve.wait_ge(bound_ready, 1)
            link(nc.vector.tensor_scalar(whm[:], bound[:, 2:3], TINY, None, ALU.max))
            link(nc.vector.reciprocal(rwhm[:], whm[:]))
            link(nc.vector.scalar_tensor_tensor(out=span[:, 0:1], in0=bound[:, 0:1], scalar=TINY, in1=bound[:, 1:2],
                                                op0=ALU.max, op1=ALU.max))
            link(nc.vector.reciprocal(span[:, 1:2], span[:, 0:1]))
            link(nc.vector.tensor_scalar(span[:, 2:3].bitcast(I32), span[:, 1:2].bitcast(I32), 0x7F800000, None,
                                         ALU.bitwise_and))
            link(nc.vector.tensor_scalar(span[:, 3:4], span[:, 2:3], GRID / 3, None, ALU.mult))

            variances(*BATCHES[0])
            means(2)
            deviations(*BATCHES[0])
            means(3)
            means(4)
            for c in range(NX):
                batch = [b for b in BATCHES if b[0] == c + 1]
                wh_out(c)
                to_grid(c)
                if batch:
                    variances(*batch[0])
                if c + 5 < NX:
                    means(c + 5)
                if batch:
                    deviations(*batch[0])
                if c == NX - 3:
                    dve.wait_ge(s1_ready, 1)
                    edges(0, 0, 0)
            s1, s2 = wh[:, :, F], wh[:, :, F + 1]
            link(nc.vector.tensor_scalar(ns2[:], s2, -1.0, None, ALU.mult))
            nc.vector.tensor_reduce(peak[:, 0:1], s2, AX_X, ALU.max)
            nc.vector.tensor_reduce(peak[:, 1:2], ns2[:], AX_X, ALU.max).then_inc(peak_ready, 1)
            for s in range(1, VLAG - 1):
                edges(0, 0, s)
            dve.wait_ge(s1_ready, NX)

            def weights(r):
                if isinstance(r, int):
                    link(nc.vector.tensor_copy(cref[:], top[:, 0:1]))
                else:
                    nc.vector.memset(first[:], 0.0)
                    link(nc.vector.tensor_scalar(cref[:], cref[:], -STEP, None, ALU.add))
                nc.vector.tensor_scalar(tcol[:], s2, cref[:], 0.0, ALU.subtract, ALU.min).then_inc(texp_in, 1)
                link(nc.vector.tensor_scalar(urow[:], s1, cref[:], None, ALU.add))
                link(nc.vector.scalar_tensor_tensor(out=mrow[:], in0=urow[:], scalar=SLOPE, in1=urow[:],
                                                    op0=ALU.mult, op1=ALU.max))
                nc.vector.tensor_tensor(drow[:, 0], urow[:], mrow[:], ALU.subtract)
                nc.vector.scalar_tensor_tensor(out=drow[:, 1], in0=urow[:], scalar=SLOPE, in1=mrow[:],
                                               op0=ALU.mult, op1=ALU.subtract).then_inc(texp_in, 1)
                dve.wait_ge(texp_out, 3 * r + 2)
                link(nc.vector.tensor_scalar(escale[:], ecol[:], rwhm[:], TOP, ALU.mult, ALU.mult))
                link(nc.vector.tensor_scalar(eden[:], ecol[:], TOP, None, ALU.mult))

            def weighted(r, k):
                for m in range(2):
                    t = slice(k * XT, (k + 1) * XT)
                    wait(dve, wlow_ready, (r * NX + k) * 2 + m - 1)
                    nc.vector.tensor_tensor(w32[m][:, :, 0:F], wh[:, t, 0:F],
                                            escale[:, m, t].unsqueeze(2).to_broadcast([P, XT, F]),
                                            ALU.mult).then_inc(w32_ready, 1)
                    nc.vector.tensor_copy(w32[m][:, :, F], eden[:, m, t]).then_inc(w32_ready, 1)

            def masks(r, g, s):
                n = (r * NG + g) * NS + s
                dve.wait_ge(step_out, n + 1)
                wait(dve, step_summed, n - NB + 1)
                last = nc.vector.tensor_scalar(posm[s % NB], sign, 0.0, None, ALU.max)
                if not (isinstance(g, int) and g == 0):
                    last = nc.vector.tensor_scalar(negm[s % NB], sign, -1.0, 0.0, ALU.mult, ALU.max)
                last.then_inc(masks_ready, 1)

            def sums_out(r, g):
                for t in range(GT):
                    wait_tile_summed(dve, r, g, t)
                    nc.vector.tensor_scalar(part[:, 1, t, :], acc[:, 2 * t + 1, 0:2 * F1],
                                            ab[:, 1, bass.ds(g * GT + t, 1)], None, ALU.mult).then_inc(neg_part, 1)

            def factors(r, g):
                q = r * NG + g
                tiles = bass.ds(g * GT, GT)
                dve.wait_ge(num_ready, q + 1)
                nc.vector.scalar_tensor_tensor(out=sel[:], in0=num[:, :, F], scalar=TAU, in1=live[:, tiles],
                                               op0=ALU.is_ge, op1=ALU.mult).then_inc(fin_chain, 1)
                nc.vector.tensor_scalar(den[:], num[:, :, F], TINY, None, ALU.max).then_inc(fin_chain, 1)
                dve.wait_ge(fin_chain, 4 * q + 2)
                nc.vector.reciprocal(rden[:], den[:]).then_inc(fin_chain, 1)
                nc.vector.tensor_tensor(live[:, tiles], live[:, tiles], sel[:], ALU.subtract).then_inc(fin_chain, 1)
                dve.wait_ge(fin_chain, 4 * q + 4)
                nc.vector.scalar_tensor_tensor(out=rs[:], in0=rden[:], scalar=whm[:], in1=sel[:],
                                               op0=ALU.mult, op1=ALU.mult)
                nc.vector.tensor_scalar(fm[:], sel[:], -1.0, first[:], ALU.mult, ALU.add).then_inc(factors_ready, 1)

            def group(r, g, more):
                for s in range(NS):
                    masks(r, g, s)
                    if isinstance(g, int) and g == 0 and s + 1 < NS:
                        weighted(r, s + 1)
                    if s + VLAG < NS:
                        edges(r, g, s + VLAG)
                    elif more:
                        edges(r, g + 1, s + VLAG - NS)
                    if not (isinstance(g, int) and g == 0):
                        if s == 0:
                            sums_out(r, g - 1)
                        if s == 2:
                            factors(r, g - 1)

            per_round = []

            def one_round(r):
                before = chain[0]
                if not isinstance(r, int):
                    earlier[0] = (r - 1) * per_round[0]
                    dve.wait_ge(out_stored, 16 * NG * r)
                    dve.wait_ge(step_summed, NG * NS * r)
                if isinstance(r, int):
                    dve.wait_ge(top_ready, 1)
                else:
                    for s in range(VLAG - 1):
                        edges(r, 0, s)
                weights(r)
                per_round.append(chain[0] - before)
                weighted(r, 0)
                edges(r, 0, VLAG - 1)
                if isinstance(r, int):
                    dve.wait_ge(mean_psum, 1)
                    nc.vector.tensor_scalar(mean[:], acc[:, 3, 0:F], 1.0 / N, None, ALU.mult).then_inc(mean_ready, 1)
                    link(nc.vector.tensor_tensor(spread[0][:], top[:, 0:1], top[:, 1:2], ALU.add))
                    link(nc.vector.tensor_scalar(spread[1][:], spread[0][:], 1.0 / STEP, None, ALU.mult))
                    link(nc.vector.tensor_copy(n_floor[:], spread[1][:]))
                    link(nc.vector.tensor_copy(spread[2][:], n_floor[:]))
                    link(nc.vector.tensor_tensor(spread[3][:], spread[2][:], spread[1][:], ALU.is_lt))
                    nc.vector.tensor_scalar(n_rounds[:], spread[2][:], spread[3][:], 1.0, ALU.add, ALU.max)\
                        .then_inc(rounds_known, 1)
                    dve.wait_ge(consts, 6)
                dve.wait_ge(texp_out, 3 * r + 3)
                groups(dve, r, group)
                sums_out(r, NG - 1)
                factors(r, NG - 1)

            rounds(dve, one_round)
            assert per_round[0] == per_round[1]

        @block.tensor
        def _(pe):
            pe.wait_ge(consts, 3)
            pe.wait_ge(w_in, 16)
            pe.wait_ge(a_in, 16)
            nc.tensor.transpose(acc[:, 0, 0:F], w_sb, ident[:]).then_inc(wx_psum, 1)
            nc.tensor.matmul(acc[:, 1, 0:2], w_sb, a_sb[:], start=True, stop=True).then_inc(wx_psum, 1)
            pe.wait_ge(wx_ready, 1)
            pe.wait_ge(wasq_ready, 1)
            nc.tensor.matmul(acc[:, 2, 0:2], ones, wasq[:], start=True, stop=True).then_inc(wasq_psum, 1)

            def turn_h(c):
                pe.wait_ge(xc_ready, c + 1)
                wait(pe, s2_ready, c - 1)
                for i in range(XT):
                    last = nc.tensor.transpose(turned[c % 2][:, i * P:(i + 1) * P], x_sb[:, c * XT + i, :], ident[:])
                last.then_inc(ht_psum, 1)

            def project(c):
                pe.wait_ge(ht_ready, c + 1)
                wait(pe, wh_ready, c)
                for i in range(XT):
                    last = nc.tensor.matmul(acc_tiles[:, i, 0:F + 2], hT[c % 2][:, i * P:(i + 1) * P], wx,
                                            start=True, stop=True)
                last.then_inc(wh_psum, 1)

            def spread_s2(c):
                pe.wait_ge(grid_ready, c + 1)
                for i in range(XT):
                    t = c * XT + i
                    last = nc.tensor.transpose(turned[c % 2][:, i * P:(i + 1) * P],
                                               on_grid[:, t:t + 1].to_broadcast([P, P]), ident[:])
                last.then_inc(s2_psum, 1)

            def turn(r, g, s):
                n = (r * NG + g) * NS + s
                pe.wait_ge(edge_ready, n + 1)
                wait(pe, step_out, n - NE + 1)
                for t in range(ST // 2):
                    for i in range(GT):
                        o = (t * GT + i) * P
                        last = nc.tensor.transpose(turned16[s % NE][:, o:o + P],
                                                   pairs[s % NE][:, (i * ST // 2 + t) * P:(i * ST // 2 + t + 1) * P],
                                                   ident16[:])
                last.then_inc(step_turned, 1)

            for c in range(NX):
                turn_h(c)
                if c:
                    spread_s2(c - 1)
                project(c)
            spread_s2(NX - 1)
            pe.wait_ge(s2_ready, NX)
            pe.wait_ge(consts, 4)
            for s in range(LAG):
                turn(0, 0, s)
            pe.wait_ge(wh_added, NX - 1)
            pe.wait_ge(wh_ready, NX)
            for i in range(XT):
                last = nc.tensor.matmul(acc[:, 3, 0:F], ones, wh_sum[NX % 2][:, i, :], start=i == 0, stop=i == XT - 1)
            last.then_inc(mean_psum, 1)
            pe.wait_ge(mean_ready, 1)

            def products(r, g, s):
                n = (r * NG + g) * NS + s
                b = s % NB
                if isinstance(g, int) and g == 0:
                    pe.wait_ge(wlow_ready, r * 2 * NX + 2 * (s * ST // XT + 1))
                    pe.wait_ge(neg_ready, r * NS + s + 1)
                pe.wait_ge(masks_ready, n + 1)
                for i in range(GT):
                    if s == 0:
                        wait(pe, pos_part, (r * NG + g - 1) * GT + i + 1)
                        wait(pe, neg_part, (r * NG + g - 1) * GT + i + 1)
                    for t in range(ST):
                        for m, mask in enumerate((posm, negm)):
                            o = (t // 2 * GT + i) * 2 * P + t % 2 * P
                            last = nc.tensor.matmul(acc[:, 2 * i + m, 0:2 * F1], mask[b][:, o:o + P],
                                                    w16[:, s * ST + t, m, :, :],
                                                    start=(s == 0 and t == 0), stop=(s == NS - 1 and t == ST - 1))
                    if s == NS - 1 and i < GT - 1:
                        last.then_inc(tile_summed[i], 1)
                last.then_inc(step_summed, 1)

            def group(r, g, more):
                for s in range(NS):
                    if s + LAG < NS:
                        turn(r, g, s + LAG)
                    elif more:
                        turn(r, g + 1, s + LAG - NS)
                    products(r, g, s)

            def one_round(r):
                if not isinstance(r, int):
                    for s in range(LAG):
                        turn(r, 0, s)
                groups(pe, r, group)

            rounds(pe, one_round)


_INS = ['x', 'adj', 'L0_gnn_W', 'L0_gnn_a']


def kernel(**inputs):
    import numpy as _np
    import concourse.bacc as _bacc
    from concourse import mybir as _mybir
    from concourse.bass_utils import run_bass_kernel_spmd as _run

    nc = _bacc.Bacc("TRN2", target_bir_lowering=False, num_devices=1)
    arrays, args = {}, []
    for name in _INS:
        v = _np.ascontiguousarray(inputs[name])
        arrays[f"in_{name}_dram"] = v
        args.append(nc.dram_tensor(f"in_{name}_dram", v.shape, _mybir.dt.from_np(v.dtype), kind="ExternalInput").ap())
    out = nc.dram_tensor("out_0_dram", inputs['x'].shape, _mybir.dt.float32, kind="ExternalOutput").ap()
    build_gat(nc, *args, out)
    r = _run(nc, [arrays], core_ids=[0])
    return r.results[0]["out_0_dram"]
```

```python
from contextlib import ExitStack

import concourse.bass as bass
from concourse import mybir

ALU = mybir.AluOpType
ACT = mybir.ActivationFunctionType
F32 = mybir.dt.float32
F16 = mybir.dt.float16
BF16 = mybir.dt.bfloat16
F8 = mybir.dt.float8e5
I32 = mybir.dt.int32
U32 = mybir.dt.uint32
AX_X = mybir.AxisListType.X
RMAX = bass.bass_isa.ReduceOp.max

P = 128
SLOPE = 0.2
LN_EPS = 1e-5
STEP = 7.5
TAU = 2.0 ** 14 * 3.3546263e-4
TOP = 2.0 ** 14
TINY = 1e-20

XT = 8
NADJ = 4
ACOLS = 1024
GT = 2
ST = ACOLS // P
NB = 2
NE = 4
GRID = 1536.0
HALF = 2.0 ** -14


def build_gat(nc, x, adj, W, a, out):
    N, F = x.shape
    NT = N // P
    NX = NT // XT
    NG = NT // GT
    NS = NT // ST
    CG = N // ACOLS
    F1 = F + 1
    SW = ST * GT * P
    BATCHES = [(0, 1)] + [(c, min(c + 2, NX)) for c in range(1, NX, 2)]
    LAG = 2
    VLAG = 3
    ACT_NEG = [s for s in range(NS) if s % 2]

    assert GT == 2 and XT == ST
    adj_v = adj.rearrange("(g p t) n -> g p t n", t=GT, p=P)
    x_v = x.rearrange("(c g p t) f -> c p g t f", g=XT // GT, t=GT, p=P)
    x_g = x.rearrange("(g p t) f -> g p t f", t=GT, p=P)
    out_v = out.rearrange("(g p t) f -> g p t f", t=GT, p=P)

    with ExitStack() as ctx:
        def sb(name, shape, dt):
            return ctx.enter_context(nc.sbuf_tensor(name, shape, dt))

        def sem(name):
            return ctx.enter_context(nc.semaphore(name))

        adj_sb = [sb(f"adj_sb{i}", [P, GT, ACOLS], I32) for i in range(NADJ)]
        s2row = sb("s2row", [P, N], F32)
        wh = sb("wh", [P, NT, F + 2], F32)
        w16_bytes = sb("w16", [P, NT * 2 * 2 * F1], F16)
        w16 = w16_bytes[:].rearrange("p (t m k f) -> p t m k f", m=2, k=2, f=F1)
        first_stage = w16_bytes[:].bitcast(F32)
        x_sb = first_stage[:, 0:NT * F].rearrange("p (t f) -> p t f", f=F)
        at = NT * F
        w_sb, wsq, ones, wx = (first_stage[:, at + i * P:at + i * P + w] for i, w in enumerate((F, F, P, F + 2)))
        at += 3 * P + F + 2
        wh_sum = [first_stage[:, at + i * XT * F:at + (i + 1) * XT * F].rearrange("p (t f) -> p t f", f=F)
                  for i in range(2)]
        at += 2 * XT * F
        ident = first_stage[:, at:at + P]
        at += P
        mu, total, total_sq, var, sd, rstd, ns2, on_grid = (first_stage[:, at + i * NT:at + (i + 1) * NT]
                                                            for i in range(8))
        at += 8 * NT
        off_grid = first_stage[:, at:at + 2 * NT].rearrange("p (t k) -> p t k", k=2)
        at += 2 * NT
        y = [first_stage[:, at + i * 2 * XT:at + (i + 1) * 2 * XT] for i in range(3)]
        shared = sb("shared", [P, 7 * SW // 2 + 2 * XT * F1], F32)

        def floats(start, *shape):
            size = 1
            for k in shape:
                size *= k
            v = shared[:, start:start + size]
            return v if len(shape) == 1 else v.rearrange("p (t f) -> p t f", f=shape[1])

        def halves(n, dt):
            return shared[:, n * SW // 2:(n + 1) * SW // 2].bitcast(dt)

        XC = XT * F
        at = SW
        sq = [floats(at + i * XC, XT, F) for i in range(2)]
        hT = [floats(at + (2 + i) * XC, XC) for i in range(2)]

        edge = [shared[:, n * SW // NE:(n + 1) * SW // NE].bitcast(F8) for n in range(NE)]
        pairs = [shared[:, n * SW // NE:(n + 1) * SW // NE].bitcast(BF16) for n in range(NE)]
        posm = [halves(n, F16) for n in (2, 3)]
        negm = [halves(n, F16) for n in (4, 5)]
        sign = [halves(6, BF16), sb("sign1", [P, SW], BF16)[:]]
        at = 7 * SW // 2
        w32 = [floats(at + i * XT * F1, XT, F1) for i in range(2)]
        part, both = (floats(at + i * 2 * GT * F1, GT, 2 * F1) for i in range(2))
        num = floats(at + 4 * GT * F1, GT, F1)
        res = floats(at + 5 * GT * F1, GT, F)
        base = floats(at + 6 * GT * F1, GT, F)
        old = sb("old", [P, GT, F], F32)
        ident16 = sb("ident16", [P, P], BF16)
        a_sb = sb("a_sb", [P, 2], F32)
        mean = sb("mean", [P, F], F32)
        peak = sb("peak", [P, 2], F32)
        top = sb("top", [P, 2], F32)
        wasq = sb("wasq", [P, 2], F32)
        rowsq = sb("rowsq", [P, 1], F32)
        norms = sb("norms", [P, 3], F32)
        bound = sb("bound", [P, 3], F32)
        span = sb("span", [P, 4], F32)
        s1odd = sb("s1odd", [P, NT], F32)
        s1_now = sb("s1_now", [P, GT], F32)
        cref = sb("cref", [P, 1], F32)
        whm = sb("whm", [P, 1], F32)
        rwhm = sb("rwhm", [P, 1], F32)
        tcol = sb("tcol", [P, NT], F32)
        ecol = sb("ecol", [P, 2, NT], F32)
        escale = sb("escale", [P, 2, NT], F32)
        eden = sb("eden", [P, 2, NT], F32)
        urow = sb("urow", [P, NT], F32)
        mrow = sb("mrow", [P, NT], F32)
        drow = sb("drow", [P, 2, NT], F32)
        ab = sb("ab", [P, 2, NT], F32)
        live = sb("live", [P, NT], F32)
        first = sb("first", [P, 1], F32)
        spread = [sb(f"spread{i}", [P, 1], F32) for i in range(4)]
        n_floor = sb("n_floor", [P, 1], I32)
        n_rounds = sb("n_rounds", [P, 1], I32)
        sel = sb("sel", [P, GT], F32)
        den = sb("den", [P, GT], F32)
        rden = sb("rden", [P, GT], F32)
        rs = sb("rs", [P, GT], F32)
        fm = sb("fm", [P, GT], F32)
        act_carrier = sb("act_carrier", [P, NS], F32)
        dve_carrier = sb("dve_carrier", [P, NS * GT], F32)

        turned = [ctx.enter_context(nc.psum_tensor(f"turned{i}", [P, XT * P], F32)) for i in range(2)]
        turned16 = [turned[n // 2][:, n % 2 * 512:(n % 2 + 1) * 512].bitcast(BF16) for n in range(NE)]
        turned8 = [turned[n // 2][:, n % 2 * 512:(n % 2 + 1) * 512].bitcast(F8) for n in range(NE)]
        acc = ctx.enter_context(nc.psum_tensor("acc", [P, 2 * GT, 512], F32))
        acc_tiles = acc[:, :, :].rearrange("p b (h w) -> p (b h) w", h=2)

        x_in = [sem(f"x_in{i}") for i in range(NX)]
        adj_in = [sem(f"adj_in{i}") for i in range(NADJ)]
        w_in = sem("w_in")
        a_in = sem("a_in")
        old_in = sem("old_in")
        out_stored = sem("out_stored")
        consts = sem("consts")
        dve_done = sem("dve_done")
        wx_psum = sem("wx_psum")
        wx_ready = sem("wx_ready")
        rowsq_ready = sem("rowsq_ready")
        wasq_ready = sem("wasq_ready")
        wasq_psum = sem("wasq_psum")
        rowtop_ready = sem("rowtop_ready")
        norms_ready = sem("norms_ready")
        bound_ready = sem("bound_ready")
        mu_ready = sem("mu_ready")
        xc_ready = sem("xc_ready")
        sq_ready = sem("sq_ready")
        var_ready = sem("var_ready")
        sd_ready = sem("sd_ready")
        ht_psum = sem("ht_psum")
        ht_ready = sem("ht_ready")
        wh_psum = sem("wh_psum")
        wh_ready = sem("wh_ready")
        grid_ready = sem("grid_ready")
        s1_ready = sem("s1_ready")
        s1_moved = sem("s1_moved")
        s2_psum = sem("s2_psum")
        s2_ready = sem("s2_ready")
        wh_added = sem("wh_added")
        mean_psum = sem("mean_psum")
        peak_ready = sem("peak_ready")
        top_ready = sem("top_ready")
        texp_in = sem("texp_in")
        texp_out = sem("texp_out")
        w32_ready = sem("w32_ready")
        whigh_ready = sem("whigh_ready")
        wlow_ready = sem("wlow_ready")
        mean_ready = sem("mean_ready")
        rounds_known = sem("rounds_known")
        step_turned = sem("step_turned")
        step_out = sem("step_out")
        edge_ready = sem("edge_ready")
        masks_ready = sem("masks_ready")
        neg_ready = sem("neg_ready")
        step_summed = sem("step_summed")
        tile_summed = [sem(f"tile_summed{i}") for i in range(GT - 1)]
        pos_part = sem("pos_part")
        both_ready = sem("both_ready")
        num_ready = sem("num_ready")
        fin_chain = sem("fin_chain")
        factors_ready = sem("factors_ready")
        pool_chain = sem("pool_chain")
        new_ready = sem("new_ready")

        block = ctx.enter_context(nc.Block())

        def wait(eng, semaphore, value):
            if not (isinstance(value, int) and value <= 0):
                eng.wait_ge(semaphore, value)

        def wait_tile_summed(eng, r, g, t):
            if t < GT - 1:
                eng.wait_ge(tile_summed[t], r * NG + g + 1)
            else:
                eng.wait_ge(step_summed, (r * NG + g + 1) * NS)

        def rounds(eng, one):
            one(0)
            eng.wait_ge(rounds_known, 1)
            n = eng.value_load(n_rounds[0:1, 0:1], min_val=1)
            with eng.If(n > 1):
                with eng.Fori(1, n) as r:
                    one(r)

        def groups(eng, r, group):
            group(r, 0, True)
            with eng.Fori(1, NG - 1) as g:
                group(r, g, True)
            group(r, NG - 1, False)

        @block.sync
        def _(sp):
            def load_adj(r, g, k):
                n = (r * NG + g) * CG + k
                wait(sp, edge_ready, n - NADJ + 1)
                sp.dma_start(adj_sb[k % NADJ][:], adj_v[g, :, :, k * ACOLS:(k + 1) * ACOLS])\
                  .then_inc(adj_in[k % NADJ], 16)

            sp.dma_start(w_sb, W).then_inc(w_in, 16)
            for c in range(NX):
                sp.dma_start(x_sb[:, c * XT:(c + 1) * XT, :].rearrange("p (g t) f -> p g t f", t=GT), x_v[c]).then_inc(x_in[c], 16)
            for k in range(NADJ):
                load_adj(0, 0, k)

            def one_round(r):
                for k in range(NADJ if isinstance(r, int) else 0, CG):
                    load_adj(r, 0, k)
                with sp.Fori(1, NG) as g:
                    for k in range(CG):
                        load_adj(r, g, k)

            rounds(sp, one_round)

        @block.gpsimd
        def _(pool):
            pool.dma_start(a_sb[:], a.rearrange("(k p) -> p k", p=P), allow_slow_non_contiguous=True).then_inc(a_in, 16)
            nc.gpsimd.memset(ident, 0.0).then_inc(consts, 1)
            nc.gpsimd.memset(ones, 1.0).then_inc(consts, 1)
            pool.wait_ge(consts, 2)
            nc.gpsimd.affine_select(out=ident, in_=ident, compare_op=ALU.not_equal, fill=1.0, base=0,
                                    pattern=[[-1, P]], channel_multiplier=1).then_inc(consts, 1)
            pool.wait_ge(consts, 3)
            nc.gpsimd.tensor_copy(ident16[:], ident).then_inc(consts, 1)
            nc.gpsimd.memset(live[:], 1.0).then_inc(consts, 1)
            nc.gpsimd.memset(first[:], 1.0).then_inc(consts, 1)

            def center(c):
                t = slice(c * XT, (c + 1) * XT)
                pool.wait_ge(mu_ready, c + 1)
                nc.gpsimd.tensor_tensor(x_sb[:, t, :], x_sb[:, t, :], mu[:, t].unsqueeze(2).to_broadcast([P, XT, F]),
                                        ALU.subtract).then_inc(xc_ready, 1)

            def add_wh(c):
                pool.wait_ge(wh_ready, c + 1)
                before = wh[:, 0:XT, 0:F] if c == 1 else wh_sum[c % 2]
                wait(pool, wh_added, c - 1)
                nc.gpsimd.tensor_tensor(wh_sum[(c + 1) % 2], before, wh[:, c * XT:(c + 1) * XT, 0:F],
                                        ALU.add).then_inc(wh_added, 1)

            for c in range(NX):
                center(c)
                if c == 1:
                    pool.wait_ge(rowsq_ready, 1)
                    nc.gpsimd.partition_all_reduce(norms[:, 2:3], rowsq[:], P, RMAX).then_inc(rowtop_ready, 1)
                if c > 3:
                    add_wh(c - 3)
            for c in range(NX - 3, NX - 1):
                add_wh(c)
            pool.wait_ge(peak_ready, 1)
            nc.gpsimd.partition_all_reduce(top[:], peak[:], P, RMAX).then_inc(top_ready, 1)
            add_wh(NX - 1)

            def finish(r, g):
                q = r * NG + g
                pool.wait_ge(both_ready, GT * (q + 1))
                nc.gpsimd.tensor_tensor(num, both[:, :, 0:F1], both[:, :, F1:2 * F1], ALU.add).then_inc(num_ready, 1)
                pool.wait_ge(fin_chain, 5 * q + 5)
                nc.gpsimd.tensor_tensor(base, mean[:].unsqueeze(1).to_broadcast([P, GT, F]),
                                        fm[:].unsqueeze(2).to_broadcast([P, GT, F]), ALU.mult).then_inc(pool_chain, 1)
                pool.wait_ge(pool_chain, 3 * q + 1)
                pool.wait_ge(old_in, 16 * (q + 1))
                nc.gpsimd.tensor_tensor(base, base, old[:], ALU.add).then_inc(pool_chain, 1)
                pool.wait_ge(num_ready, q + 1)
                pool.wait_ge(factors_ready, q + 1)
                wait(pool, out_stored, 16 * q)
                nc.gpsimd.tensor_tensor(res, num[:, :, 0:F], rs[:].unsqueeze(2).to_broadcast([P, GT, F]),
                                        ALU.mult).then_inc(pool_chain, 1)
                pool.wait_ge(pool_chain, 3 * q + 3)
                nc.gpsimd.tensor_tensor(res, res, base, ALU.add).then_inc(new_ready, 1)

            def one_round(r):
                for j in range(2 * NX):
                    k, m = j // 2, j % 2
                    t = slice(k * XT, (k + 1) * XT)
                    pool.wait_ge(whigh_ready, r * 2 * NX + j + 1)
                    nc.gpsimd.tensor_tensor(w16[:, t, m, 1, :], w32[j % 2], w16[:, t, m, 0, :],
                                            ALU.subtract).then_inc(wlow_ready, 1)
                finish(r, 0)
                with pool.Fori(1, NG) as g:
                    finish(r, g)

            rounds(pool, one_round)

        @block.scalar
        def _(act):
            def square(c):
                act.wait_ge(xc_ready, c + 1)
                wait(act, sq_ready, XT * (c - 1))
                for i in range(XT):
                    t = c * XT + i
                    nc.scalar.activation(sq[c % 2][:, i, :], x_sb[:, t, :], ACT.Square, accum_out=total_sq[:, t:t + 1])\
                        .then_inc(sq_ready, 1)

            def s2_out(c):
                act.wait_ge(s2_psum, c + 1)
                v = s2row[:, c * XT * P:(c + 1) * XT * P]
                nc.scalar.activation(v.rearrange("q (g p t) -> q g t p", t=GT, p=P),
                                     turned[c % 2][:].rearrange("q (g t p) -> q g t p", t=GT, p=P), ACT.Copy)\
                    .then_inc(s2_ready, 1)

            def root(c, end):
                act.wait_ge(var_ready, BATCHES.index((c, end)) + 1)
                nc.scalar.activation(sd[:, c * XT:end * XT], var[:, c * XT:end * XT], ACT.Sqrt).then_inc(sd_ready, 1)

            def relu_out(c):
                act.wait_ge(ht_psum, c + 1)
                wait(act, wh_psum, c - 1)
                nc.scalar.activation(hT[c % 2], turned[c % 2][:], ACT.Relu).then_inc(ht_ready, 1)

            square(0)
            relu_out(0)
            root(*BATCHES[0])
            square(1)
            act.wait_ge(norms_ready, 1)
            act.wait_ge(rowtop_ready, 1)
            nc.scalar.activation(bound[:], norms[:], ACT.Sqrt, scale=1.01 * F).then_inc(bound_ready, 1)
            for c in range(NX):
                if c:
                    relu_out(c)
                    for batch in BATCHES:
                        if batch[0] == c:
                            root(*batch)
                    s2_out(c - 1)
                if c + 2 < NX:
                    square(c + 2)
            s2_out(NX - 1)

            def step(r, g, s):
                n = (r * NG + g) * NS + s
                act.wait_ge(step_turned, n + 1)
                wait(act, masks_ready, n - NB + 1)
                if isinstance(g, int) and g == 0:
                    wait(act, neg_ready, r * len(ACT_NEG) + len([k for k in ACT_NEG if k <= s - NB]))
                nc.scalar.activation(act_carrier[:, s:s + 1], ident16[:, 0:1], ACT.Copy)
                nc.scalar.activation(sign[s % NB].rearrange("q (b k i) -> q b k i", k=2, i=P),
                                     turned8[s % NE].rearrange("q (b i k) -> q b k i", k=2, i=P), ACT.Sign)\
                    .then_inc(step_out, 1)
                if isinstance(g, int) and g == 0 and s in ACT_NEG:
                    act.wait_ge(step_out, n + 1)
                    wait(act, step_summed, n - NB + 1)
                    nc.scalar.activation(negm[s % NB], sign[s % NB], ACT.Relu, scale=-1.0).then_inc(neg_ready, 1)

            def sums_out(r, g, tiles=range(GT)):
                for t in tiles:
                    wait_tile_summed(act, r, g, t)
                    nc.scalar.activation(part[:, t, :], acc[:, 2 * t, 0:2 * F1], ACT.Copy,
                                         scale=ab[:, 0, bass.ds(g * GT + t, 1)]).then_inc(pos_part, 1)

            def load_old(r, g):
                source = x_g if isinstance(r, int) else out_v
                act.dma_start(old[:], source[g]).then_inc(old_in, 16)

            def store(r, g):
                act.wait_ge(new_ready, r * NG + g + 1)
                act.dma_start(out_v[g], res).then_inc(out_stored, 16)

            def one_round(r):
                act.wait_ge(texp_in, 2 * r + 1)
                nc.scalar.activation(ecol[:, 0], tcol[:], ACT.Exp).then_inc(texp_out, 1)
                nc.scalar.activation(ecol[:, 1], tcol[:], ACT.Exp, scale=SLOPE).then_inc(texp_out, 1)
                act.wait_ge(texp_in, 2 * r + 2)
                nc.scalar.activation(ab[:], drow[:], ACT.Exp).then_inc(texp_out, 1)
                step(r, 0, 0)
                for s in range(NS):
                    for m in range(2):
                        j = 2 * s + m
                        act.wait_ge(w32_ready, 2 * (r * 2 * NX + j + 1))
                        nc.scalar.activation(w16[:, s * XT:(s + 1) * XT, m, 0, :], w32[m], ACT.Copy)\
                            .then_inc(whigh_ready, 1)
                    if s + 1 < NS:
                        step(r, 0, s + 1)
                act.wait_ge(neg_ready, (r + 1) * len(ACT_NEG))
                with act.Fori(1, NG) as g:
                    for s in range(NS):
                        step(r, g, s)
                        if s == 0:
                            load_old(r, g - 1)
                        if s == LAG - 1:
                            sums_out(r, g - 1)
                        if s == 5:
                            store(r, g - 1)
                load_old(r, NG - 1)
                sums_out(r, NG - 1)
                store(r, NG - 1)
                act.wait_ge(out_stored, 16 * NG * (r + 1))

            rounds(act, one_round)

        @block.vector
        def _(dve):
            chain = [0]
            earlier = [0]

            def link(ins):
                chain[0] += 1
                ins.then_inc(dve_done, 1)
                dve.wait_ge(dve_done, earlier[0] + chain[0])

            def means(c):
                t = slice(c * XT, (c + 1) * XT)
                dve.wait_ge(x_in[c], 16)
                link(nc.vector.tensor_reduce(total[:, t], x_sb[:, t, :], AX_X, ALU.add))
                nc.vector.tensor_scalar(mu[:, t], total[:, t], 1.0 / F, None, ALU.mult).then_inc(mu_ready, 1)

            def variances(c, end):
                t = slice(c * XT, end * XT)
                dve.wait_ge(sq_ready, XT * end)
                nc.vector.tensor_scalar(var[:, t], total_sq[:, t], 1.0 / F, LN_EPS, ALU.mult, ALU.add)\
                    .then_inc(var_ready, 1)

            def deviations(c, end):
                t = slice(c * XT, end * XT)
                w = slice(0, (end - c) * XT)
                dve.wait_ge(sd_ready, BATCHES.index((c, end)) + 1)
                link(nc.vector.reciprocal(y[0][:, w], sd[:, t]))
                link(nc.vector.scalar_tensor_tensor(out=y[1][:, w], in0=y[0][:, w], scalar=-0.5, in1=y[0][:, w],
                                                    op0=ALU.mult, op1=ALU.mult))
                link(nc.vector.tensor_tensor(y[2][:, w], y[1][:, w], var[:, t], ALU.mult))
                link(nc.vector.scalar_tensor_tensor(out=rstd[:, t], in0=y[2][:, w], scalar=1.5, in1=y[0][:, w],
                                                    op0=ALU.add, op1=ALU.mult))

            def wh_out(c):
                t = slice(c * XT, (c + 1) * XT)
                dve.wait_ge(wh_psum, c + 1)
                nc.vector.tensor_tensor(wh[:, t, :], acc_tiles[:, :, 0:F + 2],
                                        rstd[:, t].unsqueeze(2).to_broadcast([P, XT, F + 2]), ALU.mult)\
                    .then_inc(wh_ready, 1)

            def to_grid(c):
                t = slice(c * XT, (c + 1) * XT)
                dve.wait_ge(wh_ready, c + 1)
                link(nc.vector.tensor_scalar(off_grid[:, t, :], wh[:, t, F:F + 2], span[:, 3:4], GRID, ALU.mult, ALU.add))
                nc.vector.tensor_scalar(on_grid[:, t], off_grid[:, t, 1], GRID, None, ALU.subtract)\
                    .then_inc(grid_ready, 1)
                nc.vector.tensor_scalar(s1odd[:, t], off_grid[:, t, 0], GRID, HALF, ALU.subtract, ALU.add)\
                    .then_inc(s1_ready, 1)

            def edges(r, g, s, tiles=range(GT)):
                n = (r * NG + g) * NS + s
                if s == 0 and tiles[0] == 0:
                    if isinstance(r, int) and isinstance(g, int) and g == 0:
                        dve.wait_ge(s1_ready, 1)
                    wait(dve, edge_ready, n)
                    nc.vector.tensor_scalar(s1_now[:], s1odd[:, bass.ds(g * GT, GT)], 1.0, None, ALU.mult)\
                        .then_inc(s1_moved, 1)
                if s == 0:
                    dve.wait_ge(s1_moved, r * NG + g + 1)
                if isinstance(r, int) and isinstance(g, int) and g == 0:
                    dve.wait_ge(s2_ready, s + 1)
                dve.wait_ge(adj_in[s % NADJ], 16 * ((r * NG + g) * (CG // NADJ) + s // NADJ + 1))
                wait(dve, step_turned, n - NE + 1)
                nc.vector.memset(dve_carrier[:, s * GT + tiles[0]:s * GT + tiles[0] + 1], 0.0)
                for i in tiles:
                    last = nc.vector.scalar_tensor_tensor(
                        out=edge[s % NE][:, i * ACOLS:(i + 1) * ACOLS], in0=s2row[:, s * ACOLS:(s + 1) * ACOLS],
                        scalar=s1_now[:, i:i + 1], in1=adj_sb[s % NADJ][:, i, :].bitcast(U32),
                        op0=ALU.add, op1=ALU.mult, saturate=False)
                if tiles[-1] == GT - 1:
                    last.then_inc(edge_ready, 1)

            means(0)
            means(1)
            dve.wait_ge(w_in, 16)
            link(nc.vector.tensor_tensor(wsq, w_sb, w_sb, ALU.mult))
            nc.vector.tensor_reduce(rowsq[:], wsq, AX_X, ALU.add).then_inc(rowsq_ready, 1)
            dve.wait_ge(wx_psum, 2)
            link(nc.vector.tensor_copy(wx[:, 0:F], acc[:, 0, 0:F]))
            nc.vector.tensor_copy(wx[:, F:F + 2], acc[:, 1, 0:2]).then_inc(wx_ready, 1)
            dve.wait_ge(wx_ready, 1)
            nc.vector.tensor_tensor(wasq[:], wx[:, F:F + 2], wx[:, F:F + 2], ALU.mult).then_inc(wasq_ready, 1)
            dve.wait_ge(wasq_psum, 1)
            nc.vector.tensor_copy(norms[:, 0:2], acc[:, 2, 0:2]).then_inc(norms_ready, 1)
            variances(*BATCHES[0])
            means(2)
            deviations(*BATCHES[0])
            dve.wait_ge(bound_ready, 1)
            link(nc.vector.tensor_scalar(whm[:], bound[:, 2:3], TINY, None, ALU.max))
            link(nc.vector.reciprocal(rwhm[:], whm[:]))
            link(nc.vector.scalar_tensor_tensor(out=span[:, 0:1], in0=bound[:, 0:1], scalar=TINY, in1=bound[:, 1:2],
                                                op0=ALU.max, op1=ALU.max))
            link(nc.vector.reciprocal(span[:, 1:2], span[:, 0:1]))
            link(nc.vector.tensor_scalar(span[:, 2:3].bitcast(I32), span[:, 1:2].bitcast(I32), 0x7F800000, None,
                                         ALU.bitwise_and))
            link(nc.vector.tensor_scalar(span[:, 3:4], span[:, 2:3], GRID / 3, None, ALU.mult))

            for c in range(NX):
                batch = [b for b in BATCHES if b[0] == c + 1]
                wh_out(c)
                to_grid(c)
                if batch:
                    variances(*batch[0])
                if c == 0:
                    means(3)
                if c + 4 < NX:
                    means(c + 4)
                if c:
                    edges(0, 0, (c - 1) // GT, ((c - 1) % GT,))
                if batch:
                    deviations(*batch[0])
            s1, s2 = wh[:, :, F], wh[:, :, F + 1]
            link(nc.vector.tensor_scalar(ns2, s2, -1.0, None, ALU.mult))
            nc.vector.tensor_reduce(peak[:, 0:1], s2, AX_X, ALU.max)
            nc.vector.tensor_reduce(peak[:, 1:2], ns2, AX_X, ALU.max).then_inc(peak_ready, 1)
            for k in range(NX - 1, (VLAG + 1) * GT):
                edges(0, 0, k // GT, (k % GT,))
            dve.wait_ge(s1_ready, NX)

            def weights(r):
                if isinstance(r, int):
                    link(nc.vector.tensor_copy(cref[:], top[:, 0:1]))
                else:
                    nc.vector.memset(first[:], 0.0)
                    link(nc.vector.tensor_scalar(cref[:], cref[:], -STEP, None, ALU.add))
                nc.vector.tensor_scalar(tcol[:], s2, cref[:], 0.0, ALU.subtract, ALU.min).then_inc(texp_in, 1)
                link(nc.vector.tensor_scalar(urow[:], s1, cref[:], None, ALU.add))
                link(nc.vector.scalar_tensor_tensor(out=mrow[:], in0=urow[:], scalar=SLOPE, in1=urow[:],
                                                    op0=ALU.mult, op1=ALU.max))
                nc.vector.tensor_tensor(drow[:, 0], urow[:], mrow[:], ALU.subtract)
                nc.vector.scalar_tensor_tensor(out=drow[:, 1], in0=urow[:], scalar=SLOPE, in1=mrow[:],
                                               op0=ALU.mult, op1=ALU.subtract).then_inc(texp_in, 1)
                dve.wait_ge(texp_out, 3 * r + 2)
                link(nc.vector.tensor_scalar(escale[:], ecol[:], rwhm[:], TOP, ALU.mult, ALU.mult))
                link(nc.vector.tensor_scalar(eden[:], ecol[:], TOP, None, ALU.mult))

            def weighted(r, k):
                for m in range(2):
                    t = slice(k * XT, (k + 1) * XT)
                    wait(dve, wlow_ready, (r * NX + k) * 2 + m - 1)
                    nc.vector.tensor_tensor(w32[m][:, :, 0:F], wh[:, t, 0:F],
                                            escale[:, m, t].unsqueeze(2).to_broadcast([P, XT, F]),
                                            ALU.mult).then_inc(w32_ready, 1)
                    nc.vector.tensor_copy(w32[m][:, :, F], eden[:, m, t]).then_inc(w32_ready, 1)

            def masks(r, g, s):
                n = (r * NG + g) * NS + s
                dve.wait_ge(step_out, n + 1)
                wait(dve, step_summed, n - NB + 1)
                last = nc.vector.tensor_scalar(posm[s % NB], sign[s % NB], 0.0, None, ALU.max)
                if not (isinstance(g, int) and g == 0 and s in ACT_NEG):
                    last = nc.vector.tensor_scalar(negm[s % NB], sign[s % NB], -1.0, 0.0, ALU.mult, ALU.max)
                last.then_inc(masks_ready, 1)

            def sums_out(r, g, tiles=range(GT)):
                for t in tiles:
                    wait_tile_summed(dve, r, g, t)
                    dve.wait_ge(pos_part, (r * NG + g) * GT + t + 1)
                    nc.vector.scalar_tensor_tensor(out=both[:, t, :], in0=acc[:, 2 * t + 1, 0:2 * F1],
                                                   scalar=ab[:, 1, bass.ds(g * GT + t, 1)], in1=part[:, t, :],
                                                   op0=ALU.mult, op1=ALU.add).then_inc(both_ready, 1)

            def factors(r, g):
                q = r * NG + g
                tiles = bass.ds(g * GT, GT)
                dve.wait_ge(num_ready, q + 1)
                nc.vector.scalar_tensor_tensor(out=sel[:], in0=num[:, :, F], scalar=TAU, in1=live[:, tiles],
                                               op0=ALU.is_ge, op1=ALU.mult).then_inc(fin_chain, 1)
                nc.vector.tensor_scalar(den[:], num[:, :, F], TINY, None, ALU.max).then_inc(fin_chain, 1)
                dve.wait_ge(fin_chain, 5 * q + 2)
                nc.vector.reciprocal(rden[:], den[:]).then_inc(fin_chain, 1)
                nc.vector.tensor_tensor(live[:, tiles], live[:, tiles], sel[:], ALU.subtract).then_inc(fin_chain, 1)
                nc.vector.tensor_scalar(fm[:], sel[:], -1.0, first[:], ALU.mult, ALU.add).then_inc(fin_chain, 1)
                dve.wait_ge(fin_chain, 5 * q + 5)
                nc.vector.scalar_tensor_tensor(out=rs[:], in0=rden[:], scalar=whm[:], in1=sel[:],
                                               op0=ALU.mult, op1=ALU.mult).then_inc(factors_ready, 1)
            def group(r, g, more):
                for s in range(NS):
                    masks(r, g, s)
                    if isinstance(g, int) and g == 0 and s + 1 < NS:
                        weighted(r, s + 1)
                    if isinstance(g, int) and g == 0 and s == 0:
                        pass
                    elif s + VLAG < NS:
                        edges(r, g, s + VLAG)
                    elif more:
                        edges(r, g + 1, s + VLAG - NS)
                    if not (isinstance(g, int) and g == 0):
                        if s == 0:
                            sums_out(r, g - 1)
                        if s == 2:
                            factors(r, g - 1)

            per_round = []

            def one_round(r):
                before = chain[0]
                if not isinstance(r, int):
                    earlier[0] = (r - 1) * per_round[0]
                    dve.wait_ge(out_stored, 16 * NG * r)
                    dve.wait_ge(step_summed, NG * NS * r)
                if isinstance(r, int):
                    dve.wait_ge(top_ready, 1)
                else:
                    for s in range(VLAG + 1):
                        edges(r, 0, s)
                weights(r)
                per_round.append(chain[0] - before)
                weighted(r, 0)
                if isinstance(r, int):
                    dve.wait_ge(mean_psum, 1)
                    nc.vector.tensor_scalar(mean[:], acc[:, 3, 0:F], 1.0 / N, None, ALU.mult).then_inc(mean_ready, 1)
                    link(nc.vector.tensor_tensor(spread[0][:], top[:, 0:1], top[:, 1:2], ALU.add))
                    link(nc.vector.tensor_scalar(spread[1][:], spread[0][:], 1.0 / STEP, None, ALU.mult))
                    link(nc.vector.tensor_copy(n_floor[:], spread[1][:]))
                    link(nc.vector.tensor_copy(spread[2][:], n_floor[:]))
                    link(nc.vector.tensor_tensor(spread[3][:], spread[2][:], spread[1][:], ALU.is_lt))
                    nc.vector.tensor_scalar(n_rounds[:], spread[2][:], spread[3][:], 1.0, ALU.add, ALU.max)\
                        .then_inc(rounds_known, 1)
                    dve.wait_ge(consts, 6)
                dve.wait_ge(texp_out, 3 * r + 3)
                groups(dve, r, group)
                sums_out(r, NG - 1)
                factors(r, NG - 1)

            rounds(dve, one_round)
            assert per_round[0] == per_round[1]

        @block.tensor
        def _(pe):
            pe.wait_ge(consts, 3)
            pe.wait_ge(w_in, 16)
            pe.wait_ge(a_in, 16)
            nc.tensor.transpose(acc[:, 0, 0:F], w_sb, ident).then_inc(wx_psum, 1)
            nc.tensor.matmul(acc[:, 1, 0:2], w_sb, a_sb[:], start=True, stop=True).then_inc(wx_psum, 1)
            pe.wait_ge(wx_ready, 1)
            pe.wait_ge(wasq_ready, 1)
            nc.tensor.matmul(acc[:, 2, 0:2], ones, wasq[:], start=True, stop=True).then_inc(wasq_psum, 1)

            def turn_h(c):
                pe.wait_ge(xc_ready, c + 1)
                wait(pe, s2_ready, c - 1)
                for i in range(XT):
                    last = nc.tensor.transpose(turned[c % 2][:, i * P:(i + 1) * P], x_sb[:, c * XT + i, :], ident)
                last.then_inc(ht_psum, 1)

            def project(c):
                pe.wait_ge(ht_ready, c + 1)
                wait(pe, wh_ready, c)
                for i in range(XT):
                    last = nc.tensor.matmul(acc_tiles[:, i, 0:F + 2], hT[c % 2][:, i * P:(i + 1) * P], wx,
                                            start=True, stop=True)
                last.then_inc(wh_psum, 1)

            def spread_s2(c):
                pe.wait_ge(grid_ready, c + 1)
                for i in range(XT):
                    t = c * XT + i
                    last = nc.tensor.transpose(turned[c % 2][:, i * P:(i + 1) * P],
                                               on_grid[:, t:t + 1].to_broadcast([P, P]), ident)
                last.then_inc(s2_psum, 1)

            def turn(r, g, s):
                n = (r * NG + g) * NS + s
                pe.wait_ge(edge_ready, n + 1)
                wait(pe, step_out, n - NE + 1)
                for t in range(ST // 2):
                    for i in range(GT):
                        o = (t * GT + i) * P
                        last = nc.tensor.transpose(turned16[s % NE][:, o:o + P],
                                                   pairs[s % NE][:, (i * ST // 2 + t) * P:(i * ST // 2 + t + 1) * P],
                                                   ident16[:])
                last.then_inc(step_turned, 1)

            for c in range(NX):
                turn_h(c)
                if c == 0:
                    pe.wait_ge(norms_ready, 1)
                if c:
                    spread_s2(c - 1)
                project(c)
            spread_s2(NX - 1)
            pe.wait_ge(s2_ready, NX)
            pe.wait_ge(consts, 4)
            for s in range(LAG):
                turn(0, 0, s)
            pe.wait_ge(wh_added, NX - 1)
            pe.wait_ge(wh_ready, NX)
            for i in range(XT):
                last = nc.tensor.matmul(acc[:, 3, 0:F], ones, wh_sum[NX % 2][:, i, :], start=i == 0, stop=i == XT - 1)
            last.then_inc(mean_psum, 1)
            pe.wait_ge(mean_ready, 1)

            def products(r, g, s):
                n = (r * NG + g) * NS + s
                b = s % NB
                if isinstance(g, int) and g == 0:
                    pe.wait_ge(wlow_ready, r * 2 * NX + 2 * (s * ST // XT + 1))
                    if s in ACT_NEG:
                        pe.wait_ge(neg_ready, r * len(ACT_NEG) + ACT_NEG.index(s) + 1)
                pe.wait_ge(masks_ready, n + 1)
                for i in range(GT):
                    if s == 0:
                        wait(pe, pos_part, (r * NG + g - 1) * GT + i + 1)
                        wait(pe, both_ready, (r * NG + g - 1) * GT + i + 1)
                    for t in range(ST):
                        for m, mask in enumerate((posm, negm)):
                            o = (t // 2 * GT + i) * 2 * P + t % 2 * P
                            last = nc.tensor.matmul(acc[:, 2 * i + m, 0:2 * F1], mask[b][:, o:o + P],
                                                    w16[:, s * ST + t, m, :, :],
                                                    start=(s == 0 and t == 0), stop=(s == NS - 1 and t == ST - 1))
                    if s == NS - 1 and i < GT - 1:
                        last.then_inc(tile_summed[i], 1)
                last.then_inc(step_summed, 1)

            def group(r, g, more):
                for s in range(NS):
                    if s + LAG < NS:
                        turn(r, g, s + LAG)
                    elif more:
                        turn(r, g + 1, s + LAG - NS)
                    products(r, g, s)

            def one_round(r):
                if not isinstance(r, int):
                    for s in range(LAG):
                        turn(r, 0, s)
                groups(pe, r, group)

            rounds(pe, one_round)


_INS = ['x', 'adj', 'L0_gnn_W', 'L0_gnn_a']


def kernel(**inputs):
    import numpy as _np
    import concourse.bacc as _bacc
    from concourse import mybir as _mybir
    from concourse.bass_utils import run_bass_kernel_spmd as _run

    nc = _bacc.Bacc("TRN2", target_bir_lowering=False, num_devices=1)
    arrays, args = {}, []
    for name in _INS:
        v = _np.ascontiguousarray(inputs[name])
        arrays[f"in_{name}_dram"] = v
        args.append(nc.dram_tensor(f"in_{name}_dram", v.shape, _mybir.dt.from_np(v.dtype), kind="ExternalInput").ap())
    out = nc.dram_tensor("out_0_dram", inputs['x'].shape, _mybir.dt.float32, kind="ExternalOutput").ap()
    build_gat(nc, *args, out)
    r = _run(nc, [arrays], core_ids=[0])
    return r.results[0]["out_0_dram"]
```
